# Optimizing a Trainium2 kernel written in Bass

```python
import numpy as np
import jax
import jax.numpy as jnp

def _softmax(x, axis=-1):
    return jax.nn.softmax(x, axis=axis)

def _gelu(x):
    return jax.nn.gelu(x, approximate=True)

def _silu(x):
    return jax.nn.silu(x)

def _sigmoid(x):
    return jax.nn.sigmoid(x)

def _layernorm(x, axis=-1, eps=1e-05):
    m = jnp.mean(x, axis=axis, keepdims=True)
    v = jnp.var(x, axis=axis, keepdims=True)
    return (x - m) / jnp.sqrt(v + eps)

def _scatter_add(tgt, idx, src, axis=0):
    return tgt.at[idx].add(src)

def _segment_sum(src, seg, n):
    return jax.ops.segment_sum(src, seg, n)
kernel_name = 'mk_adj_resnorm_d2_adj_r2_66ee2d'

def setup_inputs(seed: int=0):
    np.random.seed(seed)
    _w = jnp.asarray

    def _rec_inputs():
        import jax
        import jax.numpy as jnp
        _gk = jax.random.key(seed)
        x = -0.0001538 + 1 * jax.random.normal(jax.random.fold_in(_gk, 1), (64, 128, 384), jnp.float32)
        _a = jax.random.bernoulli(jax.random.fold_in(_gk, 2), 0.125, (64, 128, 128))
        _a = jnp.logical_or(_a, jnp.swapaxes(_a, -1, -2))
        _a = jnp.logical_or(_a, jnp.eye(128, dtype=bool))
        _af = _a.astype(jnp.float32)
        _af = _af * jax.random.uniform(jax.random.fold_in(_gk, 3), (64, 128, 128), jnp.float32, 0.05, 0.999992)
        adj = _af
        return (x, adj)
    x, adj = _rec_inputs()

    def _L0_gnn_setup():
        import jax, jax.numpy as jnp
        import numpy as np
        B, N, D, H = (8, 512, 384, 12)
        HD = D // H

        def _split_heads(x):
            b, n, _ = x.shape
            return x.reshape(b, n, H, HD).transpose(0, 2, 1, 3)
        key = jax.random.key(seed)
        ks = jax.random.split(key, 10)
        input_graph = jax.random.normal(ks[0], (B, N, D), dtype=jnp.float32)
        u = jax.random.uniform(ks[1], (B, N, N), dtype=jnp.float32)
        keep = jax.random.uniform(ks[2], (B, N, N)) < 0.15
        adj = jnp.where(keep, u, 0.0)
        s = 1.0 / np.sqrt(D)
        Wq = jax.random.normal(ks[3], (D, D), dtype=jnp.float32) * s
        bq = jnp.zeros((D,), dtype=jnp.float32)
        Wk = jax.random.normal(ks[4], (D, D), dtype=jnp.float32) * s
        bk = jnp.zeros((D,), dtype=jnp.float32)
        Wv = jax.random.normal(ks[5], (D, D), dtype=jnp.float32) * s
        bv = jnp.zeros((D,), dtype=jnp.float32)
        beta = jnp.asarray(0.1, dtype=jnp.float32)
        return {'input_graph': input_graph, 'adj': adj, 'Wq': Wq, 'bq': bq, 'Wk': Wk, 'bk': bk, 'Wv': Wv, 'bv': bv, 'beta': beta}
    _L0_gnn_all = _L0_gnn_setup()
    _L0_gnn_in = {k: v for k, v in _L0_gnn_all.items() if k in ('Wq', 'bq', 'Wk', 'bk', 'Wv', 'bv', 'beta')}
    del _L0_gnn_all

    def _L1_gnn_setup():
        import jax, jax.numpy as jnp
        import numpy as np
        B, S, H, L = (32, 256, 384, 2)

        def _layer_norm(z, a, b, eps=0.001):
            mu = jnp.mean(z, axis=-1, keepdims=True)
            sigma = jnp.std(z, axis=-1, keepdims=True, ddof=1)
            return (z - mu) / (sigma + eps) * a + b
        key = jax.random.key(seed)
        ks = jax.random.split(key, 6)
        hidden_state = jax.random.normal(ks[0], (B, S, H), dtype=jnp.float32)
        adjacency_matrix = (jax.random.uniform(ks[1], (B, S, S)) < 0.2).astype(jnp.float32)
        W_left = 0.05 * jax.random.normal(ks[2], (L, H, H), dtype=jnp.float32)
        W_right = 0.05 * jax.random.normal(ks[3], (L, H, H), dtype=jnp.float32)
        W_lin = 0.05 * jax.random.normal(ks[4], (L, H, H), dtype=jnp.float32)
        b_lin = jnp.zeros((L, H), dtype=jnp.float32)
        ln_a = jnp.ones((L, H), dtype=jnp.float32)
        ln_b = jnp.zeros((L, H), dtype=jnp.float32)
        return {'hidden_state': hidden_state, 'adjacency_matrix': adjacency_matrix, 'W_left': W_left, 'W_right': W_right, 'W_lin': W_lin, 'b_lin': b_lin, 'ln_a': ln_a, 'ln_b': ln_b}
    _L1_gnn_all = _L1_gnn_setup()
    _L1_gnn_in = {k: v for k, v in _L1_gnn_all.items() if k in ('W_left', 'W_right', 'W_lin', 'b_lin', 'ln_a', 'ln_b')}
    del _L1_gnn_all
    return {'x': x, 'adj': adj, 'L0_gnn_Wq': _L0_gnn_in['Wq'], 'L0_gnn_bq': _L0_gnn_in['bq'], 'L0_gnn_Wk': _L0_gnn_in['Wk'], 'L0_gnn_bk': _L0_gnn_in['bk'], 'L0_gnn_Wv': _L0_gnn_in['Wv'], 'L0_gnn_bv': _L0_gnn_in['bv'], 'L0_gnn_beta': _L0_gnn_in['beta'], 'L1_gnn_W_left': _L1_gnn_in['W_left'], 'L1_gnn_W_right': _L1_gnn_in['W_right'], 'L1_gnn_W_lin': _L1_gnn_in['W_lin'], 'L1_gnn_b_lin': _L1_gnn_in['b_lin'], 'L1_gnn_ln_a': _L1_gnn_in['ln_a'], 'L1_gnn_ln_b': _L1_gnn_in['ln_b']}

def reference(x, adj, L0_gnn_Wq, L0_gnn_bq, L0_gnn_Wk, L0_gnn_bk, L0_gnn_Wv, L0_gnn_bv, L0_gnn_beta, L1_gnn_W_left, L1_gnn_W_right, L1_gnn_W_lin, L1_gnn_b_lin, L1_gnn_ln_a, L1_gnn_ln_b):
    import jax
    import jax.numpy as jnp

    def _L0_gnn_ref(input_graph, adj, Wq, bq, Wk, bk, Wv, bv, beta):
        import jax, jax.numpy as jnp
        import numpy as np
        B, N, D, H = (8, 512, 384, 12)
        HD = D // H

        def _split_heads(x):
            b, n, _ = x.shape
            return x.reshape(b, n, H, HD).transpose(0, 2, 1, 3)
        q = _split_heads(input_graph @ Wq + bq)
        k = _split_heads(input_graph @ Wk + bk)
        v = _split_heads(input_graph @ Wv + bv)
        scores = jnp.einsum('bhqd,bhkd->bhqk', q, k) / jnp.sqrt(jnp.asarray(HD, input_graph.dtype))
        adj_e = adj[:, None, :, :]
        scores = scores + beta * adj_e
        scores = jnp.where(adj_e > 0, scores, jnp.asarray(-9000000000000000.0, scores.dtype))
        probs = jax.nn.softmax(scores, axis=-1)
        out = jnp.einsum('bhqk,bhkd->bhqd', probs, v)
        return out.transpose(0, 2, 1, 3).reshape(input_graph.shape[0], input_graph.shape[1], D)

    def _L1_gnn_ref(hidden_state, adjacency_matrix, W_left, W_right, W_lin, b_lin, ln_a, ln_b):
        import jax, jax.numpy as jnp
        import numpy as np
        B, S, H, L = (32, 256, 384, 2)

        def _layer_norm(z, a, b, eps=0.001):
            mu = jnp.mean(z, axis=-1, keepdims=True)
            sigma = jnp.std(z, axis=-1, keepdims=True, ddof=1)
            return (z - mu) / (sigma + eps) * a + b
        temper = float(np.sqrt(H))
        adj = adjacency_matrix
        adj_tri = jnp.triu(adj, k=1)
        diag_mask = jnp.triu(adj, k=0) - adj_tri
        h = hidden_state
        for l in range(L):
            m_left = jnp.einsum('bsh,oh->bso', h, W_left[l])
            m_right = jnp.einsum('bsh,oh->bso', h, W_right[l])
            u_left = jnp.einsum('bih,bjh->bij', h, m_left) / temper
            u_right = jnp.einsum('bih,bjh->bij', h, m_right) / temper
            u = u_left * adj_tri + u_left * diag_mask + u_right * jnp.swapaxes(adj_tri, 1, 2)
            delta_exp_u = jnp.exp(u) * adj
            attention = delta_exp_u / (jnp.sum(delta_exp_u, axis=2, keepdims=True) + 1e-10)
            h_lin = jnp.einsum('bsh,oh->bso', h, W_lin[l]) + b_lin[l]
            ctx = jnp.matmul(attention, h_lin)
            h = jax.nn.relu(_layer_norm(ctx, ln_a[l], ln_b[l]))
        return h
    x = _layernorm(x + _L0_gnn_ref(x, adj, L0_gnn_Wq, L0_gnn_bq, L0_gnn_Wk, L0_gnn_bk, L0_gnn_Wv, L0_gnn_bv, L0_gnn_beta), axis=-1)
    x = _layernorm(x + _L1_gnn_ref(x, adj, L1_gnn_W_left, L1_gnn_W_right, L1_gnn_W_lin, L1_gnn_b_lin, L1_gnn_ln_a, L1_gnn_ln_b), axis=-1)
    return x

_drawn_inputs = setup_inputs


def setup_inputs(seed=0):
    import zlib

    import numpy as np

    out = dict(_drawn_inputs(seed))
    spreads = {'L0_gnn_bq': (0.0, 0.271),
     'L0_gnn_bk': (0.0, 0.8),
     'L0_gnn_bv': (0.0, 0.1),
     'L1_gnn_b_lin': (0.0, 0.1),
     'L1_gnn_ln_a': (1.0, 0.2),
     'L1_gnn_ln_b': (0.0, 0.1)}
    factors = {}
    for name, (base, spread) in spreads.items():
        noise = np.random.default_rng([zlib.crc32(name.encode()), seed]).standard_normal(out[name].shape)
        drawn = base * np.exp(spread * noise) if base else spread * noise
        out[name] = jnp.asarray(drawn.astype(out[name].dtype))
    for name, factor in factors.items():
        out[name] = (out[name] * factor).astype(out[name].dtype)
    return out
```

```python
from contextlib import ExitStack

import numpy as np

import concourse.bass as bass
from concourse import mybir

F32 = mybir.dt.float32
F32R = mybir.dt.float32r
ALU = mybir.AluOpType
ACT = mybir.ActivationFunctionType
AX = mybir.AxisListType

P = 128
NB, N, D = 64, 128, 384
H = 12
HD = D // H
GB = 4
G = NB // GB
T = GB * N
DC = D // P
HPC = P // HD
TR = H // HPC
NTR = GB * HPC
L = 2
VW = HD + 1
MASKED = -9000000000000000.0
LN_EPS, L1_EPS, SUM_EPS = 1e-5, 1e-3, 1e-10


def block0_first():
    return [("A", k) for k in range(2 * DC)] + [("B", b) for b in range(GB)]


def attention_step(q):
    units = []
    if q < NTR:
        units.append(("S", q))
    if 0 <= q - 2 < NTR:
        units.append(("T", q - 2))
    if 0 <= q - 3 < NTR:
        units.append(("V", q - 3))
    return units


def block0_alone():
    units = block0_first()
    for q in range(NTR + 3):
        units += attention_step(q)
    return units + [("XL",)] + [("D", c) for c in range(DC)]


def block1_alone():
    units = [("R",)]
    for l in range(L):
        units += [("N", l, k) for k in range(2 * DC)]
        units += [("H", l, b) for b in range(GB)]
        units += [("U", l, 0), ("U", l, 1), ("E", l, 0), ("E", l, 1)]
        units += [("C", l, b) for b in range(GB)]
        units += [("Y", l)]
        if l < L - 1:
            units += [("W", c) for c in range(DC)]
    return units


def both():
    units = [("R",)]
    a = block0_first()
    n0 = [("N", 0, k) for k in range(2 * DC)]
    h0 = [("H", 0, b) for b in range(GB)]
    for x, y in zip(a[:6], n0):
        units += [x, y]
    for x, y in zip(a[6:], h0):
        units += [x, y]
    fill = {
        0: [("U", 0, 0)], 1: [("U", 0, 1)], 2: [("E", 0, 0), ("E", 0, 1)],
        3: [("C", 0, 0)], 4: [("C", 0, 1)], 5: [("C", 0, 2)], 6: [("C", 0, 3), ("Y", 0)],
        9: [("W", 0)], 10: [("W", 1), ("W", 2)],
        12: [("N", 1, 0)], 13: [("N", 1, 1)], 14: [("N", 1, 2)], 15: [("N", 1, 3)],
        16: [("N", 1, 4)], 17: [("N", 1, 5)], 18: [("H", 1, 0), ("XL",)],
    }
    for q in range(NTR + 3):
        units += attention_step(q) + fill.get(q, [])
    units += [("H", 1, 1), ("U", 1, 0), ("H", 1, 2), ("D", 0), ("U", 1, 1), ("E", 1, 0), ("D", 1), ("H", 1, 3),
              ("E", 1, 1), ("D", 2), ("C", 1, 0), ("C", 1, 1), ("C", 1, 2), ("C", 1, 3), ("Y", 1)]
    return units


def graph_blocks(nc, xT_d, xn_d, adj_d, adjT_d, wq_d, wk_d, wv_d, bq_d, bk_d, bv_d, beta_d,
                 wl_d, wr_d, wlin_d, blin_d, lna_col_d, lnb_col_d, lna_d, lnb_d, out_d):
    with ExitStack() as ctx:
        def sb(name, shape, dt=F32):
            return ctx.enter_context(nc.sbuf_tensor(name, shape, dt))

        def bank(name):
            return ctx.enter_context(nc.psum_tensor(name, [P, 512], F32))

        def sem(name):
            return ctx.enter_context(nc.semaphore(name))

        wqk = sb("wqk", [P, 2, DC, D])
        wv = sb("wv", [P, DC, D])
        w1_hi = sb("w1_hi", [P, L, 3, DC, D], F32R)
        w1_lo = sb("w1_lo", [P, L, 3, DC, D], F32R)
        bqk = sb("bqk", [P, 2, DC])
        bv_b = sb("bv_b", [P, D])
        blin_b = sb("blin_b", [P, L, D])
        lna_b = sb("lna_b", [P, D])
        lnb_b = sb("lnb_b", [P, D])
        lna_c = sb("lna_c", [P, DC])
        lnb_c = sb("lnb_c", [P, DC])
        beta = sb("beta", [P, 1])
        ident = sb("ident", [P, P])
        half = sb("half", [P, 2, GB])

        xT = sb("xT", [P, DC, T])
        xn = sb("xn", [P, GB, D])
        adj = sb("adj", [P, GB, N])
        bias = sb("bias", [P, GB, N])
        qkT = sb("qkT", [P, 2, DC, T])
        v = sb("v", [P, GB, H, VW])
        sm = sb("sm", [P, 2, TR, N])
        nmax = sb("nmax", [P, 2, TR])
        pr = sb("pr", [P, 2, TR, N])
        prT = sb("prT", [P, 2, TR, N])
        rden = sb("rden", [P, 2, H])
        att = sb("att", [P, 2, D])
        st0 = sb("st0", [P, GB, 6])
        mv0 = sb("mv0", [P, GB, 2])
        ve0 = sb("ve0", [P, GB])
        rs0 = sb("rs0", [P, GB])

        x1T_hi = sb("x1T_hi", [P, DC, T], F32R)
        x1T_lo = sb("x1T_lo", [P, DC, T], F32R)
        h1T_hi = sb("h1T_hi", [P, DC, T], F32R)
        h1T_lo = sb("h1T_lo", [P, DC, T], F32R)
        hT = sb("hT", [P, DC, T])
        x1 = sb("x1", [P, GB, D])
        adj1 = sb("adj1", [P, 2, GB, N])
        tri = sb("tri", [P, GB, 2, N])
        nT = sb("nT", [P, DC, 2, T])
        hl = sb("hl", [P, GB, D + 1])
        uw = sb("uw", [P, 2, 2, N])
        uc = sb("uc", [P, GB, N])
        cs = sb("cs", [P, GB, D + 1])
        st1 = sb("st1", [P, GB, 6])
        mv1 = sb("mv1", [P, GB, 2])
        sc = sb("sc", [P, 5, GB])
        stf = sb("stf", [P, GB, 6])
        mvf = sb("mvf", [P, GB, 2])
        rsf = sb("rsf", [P, 2, GB])

        bank_p0, bank_s0, bank_s1, bank_t, bank_o, bank_p1, bank_u, bank_c = (
            bank(n) for n in ("bank_p0", "bank_s0", "bank_s1", "bank_t", "bank_o", "bank_p1", "bank_u", "bank_c"))
        bank_s = [bank_s0, bank_s1]
        d_banks = [bank_t, bank_p0, bank_t]
        w_banks = [bank_u, bank_c, bank_u]

        ld_w0 = sem("ld_w0")
        ld_w1 = sem("ld_w1")
        ld_w1s = [sem(f"ld_w1s{i}") for i in range(3 * L)]
        w1_hi_done = sem("w1_hi_done")
        w1_lo_done = sem("w1_lo_done")
        const_done = sem("const_done")
        ident_zero = sem("ident_zero")
        ld_xT = sem("ld_xT")
        ld_xn = sem("ld_xn")
        ld_adj = sem("ld_adj")
        ld_adj1 = sem("ld_adj1")
        st_out = sem("st_out")
        qk_mm = sem("qk_mm")
        qk_sb = sem("qk_sb")
        v_mm = sem("v_mm")
        v_sb = sem("v_sb")
        pen_ok = sem("pen_ok")
        bias_ok = sem("bias_ok")
        s_mm = sem("s_mm")
        s_sb = sem("s_sb")
        nmax_ok = sem("nmax_ok")
        exp_ok = sem("exp_ok")
        pt_mm = sem("pt_mm")
        pt_sb = sem("pt_sb")
        o_mm = sem("o_mm")
        rden_ok = sem("rden_ok")
        att_ok = sem("att_ok")
        res0_ok = sem("res0_ok")
        st0_ok = sem("st0_ok")
        mv0_ok = sem("mv0_ok")
        ve0_ok = sem("ve0_ok")
        rs0_ok = sem("rs0_ok")
        x1_ok = sem("x1_ok")
        x1T_mm = sem("x1T_mm")
        x1T_hi_ok = sem("x1T_hi_ok")
        x1T_lo_ok = sem("x1T_lo_ok")
        x1_kept = sem("x1_kept")
        hT0_ok = sem("hT0_ok")
        tri_ok = sem("tri_ok")
        n_mm = sem("n_mm")
        n_sb = sem("n_sb")
        hl_mm = sem("hl_mm")
        hl_sb = sem("hl_sb")
        u_mm = sem("u_mm")
        u_sb = sem("u_sb")
        ut_ok = sem("ut_ok")
        ue_ok = sem("ue_ok")
        e_ok = sem("e_ok")
        c_mm = sem("c_mm")
        c_sb = sem("c_sb")
        st1_ok = sem("st1_ok")
        mv1_ok = sem("mv1_ok")
        sc_ok = sem("sc_ok")
        sd_ok = sem("sd_ok")
        y_ok = sem("y_ok")
        yT_mm = sem("yT_mm")
        h1_ok = sem("h1_ok")
        h1_hi_ok = sem("h1_hi_ok")
        h1_lo_ok = sem("h1_lo_ok")
        fa_ok = sem("fa_ok")
        fb_ok = sem("fb_ok")
        res1_ok = sem("res1_ok")
        stf_ok = sem("stf_ok")
        mvf_ok = sem("mvf_ok")
        vef_ok = sem("vef_ok")
        rsf_ok = sem("rsf_ok")
        carrier = sem("carrier")
        out_ok = sem("out_ok")

        def some(value):
            return not isinstance(value, int) or value > 0

        def alone(eng):
            eng.sem_inc(carrier, 1)

        block = ctx.enter_context(nc.Block())

        stage = [nT[:, :, 0, 0:D], nT[:, :, 1, 0:D], hT[:, :, 0:D]]
        w1_src = [w[l].rearrange("(c p) n -> p c n", p=P) for l in range(L) for w in (wl_d, wr_d, wlin_d)]

        def over_iterations(eng, unit):
            for u in block0_alone():
                unit(u, 0, None)
            for u in both():
                unit(u, 1, 0)
            with eng.Fori(2, G) as g:
                for u in both():
                    unit(u, g, g - 1)
            for u in block1_alone():
                unit(u, None, G - 1)

        @block.sync
        def _(eng):
            def load_block0(g, at):
                if some(n := g * GB):
                    eng.wait_ge(v_mm, n)
                alone(eng)
                eng.dma_start(xT[:, :, :], xT_d[at]).then_inc(ld_xT, 16)
                if some(n := g * NTR):
                    eng.wait_ge(s_sb, n)
                alone(eng)
                eng.dma_start(adj[:, :, :], adj_d[at]).then_inc(ld_adj, 16)

            def load_xn(g, at):
                if some(n := g):
                    eng.wait_ge(x1_kept, n)
                alone(eng)
                if some(n := g * DC):
                    eng.wait_ge(x1T_mm, n)
                alone(eng)
                eng.dma_start(xn[:, :, :], xn_d[at]).then_inc(ld_xn, 16)

            def load_block1(h, at):
                if some(n := h * (2 * L)):
                    eng.wait_ge(e_ok, n)
                alone(eng)
                if some(n := h * 2):
                    eng.wait_ge(tri_ok, n)
                alone(eng)
                eng.dma_start(adj1[:, 0, :, :], adj_d[at]).then_inc(ld_adj1, 16)
                eng.dma_start(adj1[:, 1, :, :], adjT_d[at]).then_inc(ld_adj1, 16)

            def store(h, at):
                eng.wait_ge(out_ok, (h + 1) * GB)
                alone(eng)
                eng.dma_start(out_d[at], cs[:, :, 0:D]).then_inc(st_out, 16)

            eng.dma_start(xT[:, :, :], xT_d[0]).then_inc(ld_xT, 16)
            for i, w in enumerate((wq_d, wk_d)):
                eng.dma_start(wqk[:, i, :, :], w.rearrange("(c p) n -> p c n", p=P)).then_inc(ld_w0, 16)
            eng.dma_start(bqk[:, 0, :], bq_d).then_inc(ld_w0, 16)
            eng.dma_start(bqk[:, 1, :], bk_d).then_inc(ld_w0, 16)
            eng.dma_start(wv[:, :, :], wv_d.rearrange("(c p) n -> p c n", p=P)).then_inc(ld_w0, 16)
            eng.dma_start(bv_b[:, :], bv_d.partition_broadcast(P)).then_inc(ld_w0, 16)
            eng.dma_start(beta[:, :], beta_d.partition_broadcast(P)).then_inc(ld_w0, 16)
            eng.dma_start(adj[:, :, :], adj_d[0]).then_inc(ld_adj, 16)
            for i in range(3):
                eng.dma_start(stage[i], w1_src[i]).then_inc(ld_w1s[i], 16)
            load_xn(0, 0)
            for l in range(L):
                eng.dma_start(blin_b[:, l, :], blin_d[l].partition_broadcast(P)).then_inc(ld_w1, 16)
            eng.dma_start(lna_b[:, :], lna_d.partition_broadcast(P)).then_inc(ld_w1, 16)
            eng.dma_start(lnb_b[:, :], lnb_d.partition_broadcast(P)).then_inc(ld_w1, 16)
            eng.dma_start(lna_c[:, :], lna_col_d).then_inc(ld_w1, 16)
            eng.dma_start(lnb_c[:, :], lnb_col_d).then_inc(ld_w1, 16)
            for i in range(3, 3 * L):
                eng.wait_ge(w1_lo_done, i - 2)
                eng.dma_start(stage[i - 3], w1_src[i]).then_inc(ld_w1s[i], 16)
            load_block0(1, 1)
            load_block1(0, 0)
            load_xn(1, 1)
            with eng.Fori(2, G) as g:
                load_block0(g, g)
                store(g - 2, g - 2)
                load_block1(g - 1, g - 1)
                load_xn(g, g)
            store(G - 2, G - 2)
            load_block1(G - 1, G - 1)
            store(G - 1, G - 1)
            eng.wait_ge(st_out, 16 * G)

        @block.gpsimd
        def _(eng):
            eng.memset(ident[:, :], 0.0).then_inc(ident_zero, 1)
            eng.memset(half[:, 0, :], -0.5).then_inc(const_done, 1)
            eng.memset(half[:, 1, :], 0.5).then_inc(const_done, 1)
            eng.memset(v[:, :, :, HD:VW], 1.0).then_inc(const_done, 1)
            eng.memset(hl[:, :, D:D + 1], 1.0).then_inc(const_done, 1)
            eng.wait_ge(ident_zero, 1)
            eng.affine_select(out=ident[:, :], in_=ident[:, :], compare_op=ALU.not_equal, fill=1.0,
                              base=0, pattern=[[-1, P]], channel_multiplier=1).then_inc(const_done, 1)
            for i in range(3 * L):
                eng.wait_ge(w1_hi_done, i + 1)
                eng.tensor_tensor(w1_lo[:, i // 3, i % 3, :, :], stage[i % 3],
                                  w1_hi[:, i // 3, i % 3, :, :].bitcast(F32), ALU.subtract).then_inc(w1_lo_done, 1)

            def unit(u, g, h):
                if u[0] == "V" and u[1] % HPC == HPC - 1:
                    b = u[1] // HPC
                    eng.wait_ge(att_ok, g * GB + b + 1)
                    eng.wait_ge(ld_xn, (g + 1) * 16)
                    eng.tensor_tensor(xn[:, b, :], xn[:, b, :], att[:, b % 2, :], ALU.add).then_inc(res0_ok, 1)
                elif u[0] == "XL":
                    eng.wait_ge(ve0_ok, g + 1)
                    if some(n := g * GB):
                        eng.wait_ge(x1_ok, n)
                    eng.tensor_tensor(rs0[:, :], ve0[:, :], half[:, 0, :], ALU.pow).then_inc(rs0_ok, 1)
                elif u[0] == "R":
                    eng.wait_ge(x1T_lo_ok, (h + 1) * DC)
                    if some(n := h * (2 * L)):
                        eng.wait_ge(u_mm, n)
                    eng.tensor_tensor(hT[:, :, :], x1T_hi[:, :, :].bitcast(F32), x1T_lo[:, :, :].bitcast(F32),
                                      ALU.add).then_inc(hT0_ok, 1)
                    eng.wait_ge(ld_adj1, (h + 1) * 32)
                    if some(n := h * (2 * L)):
                        eng.wait_ge(u_sb, n)
                    alone(eng)
                    eng.affine_select(out=tri[:, :, 0, :], in_=adj1[:, 1, :, :], compare_op=ALU.is_ge, fill=0.0,
                                      base=0, pattern=[[0, GB], [-1, N]], channel_multiplier=1).then_inc(tri_ok, 1)
                    eng.affine_select(out=tri[:, :, 1, :], in_=adj1[:, 0, :, :], compare_op=ALU.is_gt, fill=0.0,
                                      base=0, pattern=[[0, GB], [1, N]], channel_multiplier=-1).then_inc(tri_ok, 1)
                    if some(n := h * GB):
                        eng.wait_ge(res1_ok, n)
                    eng.wait_ge(x1_ok, (h + 1) * GB)
                    alone(eng)
                    eng.tensor_copy(x1[:, :, :], xn[:, :, :]).then_inc(x1_kept, 1)
                elif u[0] == "W":
                    c = u[1]
                    eng.wait_ge(h1_hi_ok, h * DC + c + 1)
                    eng.tensor_tensor(h1T_lo[:, c, :], hT[:, c, :], h1T_hi[:, c, :].bitcast(F32),
                                      ALU.subtract).then_inc(h1_lo_ok, 1)
                elif u[0] == "Y":
                    l = u[1]
                    eng.wait_ge(sc_ok, h * (4 * L) + 4 * l + 1)
                    eng.tensor_tensor(sc[:, 1, :], sc[:, 0, :], half[:, 1, :], ALU.pow).then_inc(sd_ok, 1)
                    if l == L - 1:
                        eng.wait_ge(vef_ok, h + 1)
                        eng.tensor_tensor(rsf[:, 1, :], rsf[:, 0, :], half[:, 0, :], ALU.pow).then_inc(rsf_ok, 1)

            eng.wait_ge(const_done, 5)
            over_iterations(eng, unit)

        @block.scalar
        def _(eng):
            for i in range(3 * L):
                eng.wait_ge(ld_w1s[i], 16)
                eng.activation(w1_hi[:, i // 3, i % 3, :, :], stage[i % 3], ACT.Copy).then_inc(w1_hi_done, 1)
                if i == 2:
                    eng.wait_ge(ld_w0, 7 * 16)

            def unit(u, g, h):
                if u[0] == "A":
                    i, c = divmod(u[1], DC)
                    eng.wait_ge(qk_mm, g * (2 * DC) + u[1] + 1)
                    if some(n := g * NTR):
                        eng.wait_ge(s_mm, n)
                    eng.activation(qkT[:, i, c, :], bank_p0[:, :], ACT.Identity,
                                   bias=bqk[:, i, c:c + 1]).then_inc(qk_sb, 1)
                elif u[0] == "S":
                    q = u[1]
                    eng.wait_ge(nmax_ok, g * NTR + q + 1)
                    if some(n := g * NTR + q - 1):
                        eng.wait_ge(pt_mm, n)
                    for j in range(TR):
                        last = eng.activation(pr[:, q % 2, j, :], sm[:, q % 2, j, :], ACT.Exp,
                                              bias=nmax[:, q % 2, j:j + 1])
                    last.then_inc(exp_ok, 1)
                elif u[0] == "T":
                    q = u[1]
                    eng.wait_ge(pt_mm, g * NTR + q + 1)
                    if some(n := g * NTR + q - 1):
                        eng.wait_ge(o_mm, n)
                    eng.activation(prT[:, q % 2, :, :], bank_t[:, 0:TR * N], ACT.Copy).then_inc(pt_sb, 1)
                elif u[0] == "D":
                    c = u[1]
                    eng.wait_ge(x1T_mm, g * DC + c + 1)
                    if some(n := g * (L * GB) + GB - L * GB):
                        eng.wait_ge(hl_mm, n)
                    eng.activation(x1T_hi[:, c, :], d_banks[c][:, :], ACT.Copy).then_inc(x1T_hi_ok, 1)
                elif u[0] == "N":
                    l, k = u[1], u[2]
                    side, c = divmod(k, DC)
                    eng.wait_ge(n_mm, h * (2 * DC * L) + 2 * DC * l + k + 1)
                    if some(n := h * (2 * L) + 2 * l):
                        eng.wait_ge(u_mm, n)
                    eng.activation(nT[:, c, side, :], bank_p1[:, :], ACT.Copy).then_inc(n_sb, 1)
                elif u[0] == "E":
                    l, p = u[1], u[2]
                    eng.wait_ge(ut_ok, h * (2 * L) + 2 * l + p + 1)
                    eng.activation(uc[:, 2 * p:2 * p + 2, :], uc[:, 2 * p:2 * p + 2, :], ACT.Exp,
                                   scale=float(1.0 / np.sqrt(D))).then_inc(ue_ok, 1)
                elif u[0] == "C":
                    l, b = u[1], u[2]
                    eng.wait_ge(c_mm, h * (GB * L) + GB * l + b + 1)
                    if l == 0:
                        if some(n := h * 16):
                            eng.wait_ge(st_out, n)
                    else:
                        eng.wait_ge(yT_mm, (h + 1) * DC)
                    eng.activation(cs[:, b, :], bank_c[:, 0:D + 1], ACT.Copy).then_inc(c_sb, 1)
                elif u[0] == "W":
                    c = u[1]
                    eng.wait_ge(yT_mm, h * DC + c + 1)
                    eng.wait_ge(u_mm, h * (2 * L) + 2)
                    eng.activation(hT[:, c, :], w_banks[c][:, :], ACT.Relu, bias=lnb_c[:, c:c + 1],
                                   scale=lna_c[:, c:c + 1]).then_inc(h1_ok, 1)

            over_iterations(eng, unit)

        @block.vector
        def _(eng):
            def make_bias(g):
                eng.wait_ge(ld_adj, (g + 1) * 16)
                if some(n := g * NTR):
                    eng.wait_ge(s_sb, n)
                eng.tensor_scalar(bias[:, :, :], adj[:, :, :], 0.0, MASKED, ALU.is_le, ALU.mult).then_inc(pen_ok, 1)
                eng.wait_ge(pen_ok, g + 1)
                eng.scalar_tensor_tensor(out=bias[:, :, :], in0=adj[:, :, :], scalar=beta[:, 0:1], in1=bias[:, :, :],
                                         op0=ALU.mult, op1=ALU.add).then_inc(bias_ok, 1)

            def unit(u, g, h):
                if u[0] == "A" and u[1] == 2:
                    make_bias(g)
                elif u[0] == "B":
                    b = u[1]
                    eng.wait_ge(v_mm, g * GB + b + 1)
                    if some(n := g * NTR + HPC * (b + 1) - NTR):
                        eng.wait_ge(o_mm, n)
                    eng.tensor_tensor(v[:, b, :, 0:HD], bank_p0[:, 0:D].rearrange("p (h d) -> p h d", h=H),
                                      bv_b[:, :].rearrange("p (h d) -> p h d", h=H), ALU.add).then_inc(v_sb, 1)
                elif u[0] == "S":
                    q = u[1]
                    b = q // HPC
                    eng.wait_ge(s_mm, g * NTR + q + 1)
                    if some(n := g * NTR + q - 1):
                        eng.wait_ge(exp_ok, n)
                    eng.wait_ge(bias_ok, g + 1)
                    eng.scalar_tensor_tensor(
                        out=sm[:, q % 2, :, :], in0=bank_s[q % 2][:, 0:TR * N].rearrange("p (t n) -> p t n", t=TR),
                        scalar=float(1.0 / np.sqrt(HD)),
                        in1=bias[:, b:b + 1, :].to_broadcast([P, TR, N]), op0=ALU.mult, op1=ALU.add).then_inc(s_sb, 1)
                    eng.wait_ge(s_sb, g * NTR + q + 1)
                    eng.tensor_reduce(nmax[:, q % 2, :], sm[:, q % 2, :, :], AX.X, ALU.max,
                                      negate=True).then_inc(nmax_ok, 1)
                elif u[0] == "V":
                    q = u[1]
                    b = q // HPC
                    if q % HPC == HPC - 1:
                        o = bank_o[:, 0:H * VW].rearrange("p (h d) -> p h d", h=H)
                        eng.wait_ge(o_mm, g * NTR + q + 1)
                        eng.reciprocal(rden[:, b % 2, :], o[:, :, HD]).then_inc(rden_ok, 1)
                        eng.wait_ge(rden_ok, g * GB + b + 1)
                        if some(n := g * GB + b - 1):
                            eng.wait_ge(res0_ok, n)
                        eng.tensor_tensor(att[:, b % 2, :].rearrange("p (h d) -> p h d", h=H), o[:, :, 0:HD],
                                          rden[:, b % 2, :].unsqueeze(2).to_broadcast([P, H, HD]),
                                          ALU.mult).then_inc(att_ok, 1)
                    if b > 0 and q % HPC == 1:
                        stats0(g, b - 1)
                elif u[0] == "XL":
                    stats0(g, GB - 1)
                    for b in range(GB):
                        eng.wait_ge(st0_ok, g * GB + b + 1)
                        alone(eng)
                        last = eng.bn_aggr(mv0[:, b, :], st0[:, b, :])
                    last.then_inc(mv0_ok, 1)
                    eng.wait_ge(mv0_ok, g + 1)
                    eng.tensor_scalar(ve0[:, :], mv0[:, :, 1], LN_EPS, None, ALU.add).then_inc(ve0_ok, 1)
                elif u[0] == "D":
                    c = u[1]
                    if c == 0:
                        eng.wait_ge(rs0_ok, g + 1)
                        for b in range(GB):
                            eng.tensor_scalar(xn[:, b, :], xn[:, b, :], mv0[:, b, 0:1], rs0[:, b:b + 1],
                                              ALU.subtract, ALU.mult).then_inc(x1_ok, 1)
                    eng.wait_ge(x1T_hi_ok, g * DC + c + 1)
                    eng.tensor_tensor(x1T_lo[:, c, :], d_banks[c][:, :], x1T_hi[:, c, :].bitcast(F32),
                                      ALU.subtract).then_inc(x1T_lo_ok, 1)
                elif u[0] == "H":
                    l, b = u[1], u[2]
                    eng.wait_ge(hl_mm, h * (GB * L) + GB * l + b + 1)
                    if some(n := h * (GB * L) + GB * (l - 1) + b + 1):
                        eng.wait_ge(c_mm, n)
                    eng.tensor_tensor(hl[:, b, 0:D], bank_p1[:, 0:D], blin_b[:, l, :], ALU.add).then_inc(hl_sb, 1)
                elif u[0] == "U":
                    l, p = u[1], u[2]
                    eng.wait_ge(u_mm, h * (2 * L) + 2 * l + p + 1)
                    eng.wait_ge(tri_ok, (h + 1) * 2)
                    if some(n := h * (2 * L) + 2 * l + p):
                        eng.wait_ge(ut_ok, n)
                    eng.tensor_tensor(uw[:, :, :, :], bank_u[:, :].rearrange("p (b s n) -> p b s n", b=2, s=2),
                                      tri[:, 2 * p:2 * p + 2, :, :], ALU.mult).then_inc(u_sb, 1)
                    eng.wait_ge(u_sb, h * (2 * L) + 2 * l + p + 1)
                    if some(n := h * (GB * L) + GB * (l - 1) + 2 * p + 2):
                        eng.wait_ge(c_mm, n)
                    eng.tensor_tensor(uc[:, 2 * p:2 * p + 2, :], uw[:, :, 0, :], uw[:, :, 1, :],
                                      ALU.add).then_inc(ut_ok, 1)
                elif u[0] == "E":
                    l, p = u[1], u[2]
                    eng.wait_ge(ue_ok, h * (2 * L) + 2 * l + p + 1)
                    eng.tensor_tensor(uc[:, 2 * p:2 * p + 2, :], uc[:, 2 * p:2 * p + 2, :],
                                      adj1[:, 1, 2 * p:2 * p + 2, :], ALU.mult).then_inc(e_ok, 1)
                elif u[0] == "C":
                    l, b = u[1], u[2]
                    eng.wait_ge(c_sb, h * (GB * L) + GB * l + b + 1)
                    eng.bn_stats(st1[:, b, :], cs[:, b, 0:D]).then_inc(st1_ok, 1)
                elif u[0] == "Y":
                    context_norm(u[1], h)
                elif u[0] == "W":
                    c = u[1]
                    eng.wait_ge(h1_ok, h * DC + c + 1)
                    if some(n := h * (L * GB)):
                        eng.wait_ge(hl_mm, n)
                    eng.tensor_copy(h1T_hi[:, c, :], hT[:, c, :]).then_inc(h1_hi_ok, 1)

            def stats0(g, b):
                eng.wait_ge(res0_ok, g * GB + b + 1)
                eng.bn_stats(st0[:, b, :], xn[:, b, :]).then_inc(st0_ok, 1)

            def context_norm(l, h):
                eng.wait_ge(st1_ok, h * (GB * L) + GB * l + GB)
                alone(eng)
                for b in range(GB):
                    last = eng.bn_aggr(mv1[:, b, :], st1[:, b, :])
                last.then_inc(mv1_ok, 1)
                eng.wait_ge(mv1_ok, h * L + l + 1)
                eng.tensor_scalar(sc[:, 0, :], mv1[:, :, 1], float(D) / (D - 1), None, ALU.mult).then_inc(sc_ok, 1)
                eng.tensor_scalar(sc[:, 2, :], cs[:, :, D], SUM_EPS, None, ALU.add).then_inc(sc_ok, 1)
                eng.wait_ge(sc_ok, h * (4 * L) + 4 * l + 2)
                eng.wait_ge(sd_ok, h * L + l + 1)
                eng.scalar_tensor_tensor(out=sc[:, 3, :], in0=sc[:, 2, :], scalar=L1_EPS, in1=sc[:, 1, :],
                                         op0=ALU.mult, op1=ALU.add).then_inc(sc_ok, 1)
                eng.wait_ge(sc_ok, h * (4 * L) + 4 * l + 3)
                eng.reciprocal(sc[:, 4, :], sc[:, 3, :]).then_inc(sc_ok, 1)
                eng.wait_ge(sc_ok, h * (4 * L) + 4 * l + 4)
                if l < L - 1:
                    for b in range(GB):
                        eng.tensor_scalar(cs[:, b, 0:D], cs[:, b, 0:D], mv1[:, b, 0:1], sc[:, 4, b:b + 1],
                                          ALU.subtract, ALU.mult).then_inc(y_ok, 1)
                    return
                for b in range(GB):
                    eng.scalar_tensor_tensor(out=cs[:, b, 0:D], in0=cs[:, b, 0:D], scalar=mv1[:, b, 0:1],
                                             in1=lna_b[:, :], op0=ALU.subtract, op1=ALU.mult).then_inc(fa_ok, 1)
                for b in range(GB):
                    eng.wait_ge(fa_ok, h * GB + b + 1)
                    eng.scalar_tensor_tensor(out=cs[:, b, 0:D], in0=cs[:, b, 0:D], scalar=sc[:, 4, b:b + 1],
                                             in1=lnb_b[:, :], op0=ALU.mult, op1=ALU.add).then_inc(fb_ok, 1)
                for b in range(GB):
                    eng.wait_ge(fb_ok, h * GB + b + 1)
                    eng.wait_ge(x1_kept, h + 1)
                    eng.scalar_tensor_tensor(out=cs[:, b, 0:D], in0=cs[:, b, 0:D], scalar=0.0,
                                             in1=x1[:, b, :], op0=ALU.max, op1=ALU.add).then_inc(res1_ok, 1)
                for b in range(GB):
                    eng.wait_ge(res1_ok, h * GB + b + 1)
                    eng.bn_stats(stf[:, b, :], cs[:, b, 0:D]).then_inc(stf_ok, 1)
                for b in range(GB):
                    eng.wait_ge(stf_ok, h * GB + b + 1)
                    alone(eng)
                    last = eng.bn_aggr(mvf[:, b, :], stf[:, b, :])
                last.then_inc(mvf_ok, 1)
                eng.wait_ge(mvf_ok, h + 1)
                eng.tensor_scalar(rsf[:, 0, :], mvf[:, :, 1], LN_EPS, None, ALU.add).then_inc(vef_ok, 1)
                eng.wait_ge(rsf_ok, h + 1)
                for b in range(GB):
                    eng.tensor_scalar(cs[:, b, 0:D], cs[:, b, 0:D], mvf[:, b, 0:1], rsf[:, 1, b:b + 1],
                                      ALU.subtract, ALU.mult).then_inc(out_ok, 1)

            eng.wait_ge(ld_w0, 7 * 16)
            eng.wait_ge(ld_w1, 6 * 16)
            over_iterations(eng, unit)

        @block.tensor
        def _(eng):
            def split_product(out, w_hi, w_lo, x_hi, x_lo):
                for c in range(DC):
                    for n, (a, b) in enumerate(((w_hi, x_hi), (w_hi, x_lo), (w_lo, x_hi))):
                        last = eng.matmul(out, a(c), b(c), start=(c == 0 and n == 0), stop=(c == DC - 1 and n == 2))
                return last

            def unit(u, g, h):
                if u[0] == "A":
                    i, m = divmod(u[1], DC)
                    if u[1] == 0:
                        eng.wait_ge(ld_xT, (g + 1) * 16)
                        if some(n := g * DC - 1):
                            eng.wait_ge(x1T_lo_ok, n)
                    if some(n := g * (2 * DC) + u[1]):
                        eng.wait_ge(qk_sb, n)
                    for c in range(DC):
                        last = eng.matmul(bank_p0[:, :], wqk[:, i, c, m * P:(m + 1) * P], xT[:, c, :],
                                          start=(c == 0), stop=(c == DC - 1))
                    last.then_inc(qk_mm, 1)
                elif u[0] == "B":
                    b = u[1]
                    eng.wait_ge(qk_sb, (g + 1) * (2 * DC))
                    if some(n := g * GB + b):
                        eng.wait_ge(v_sb, n)
                    for c in range(DC):
                        last = eng.matmul(bank_p0[:, 0:D], xT[:, c, b * N:(b + 1) * N], wv[:, c, :],
                                          start=(c == 0), stop=(c == DC - 1))
                    last.then_inc(v_mm, 1)
                elif u[0] == "S":
                    q = u[1]
                    b, j = divmod(q, HPC)
                    rows = slice(j * HD, (j + 1) * HD)
                    eng.wait_ge(qk_sb, (g + 1) * (2 * DC))
                    if some(n := g * NTR + q - 1):
                        eng.wait_ge(s_sb, n)
                    for c in range(TR):
                        last = eng.matmul(bank_s[q % 2][:, c * N:(c + 1) * N], qkT[rows, 0, c, b * N:(b + 1) * N],
                                          qkT[rows, 1, c, b * N:(b + 1) * N], start=True, stop=True)
                    last.then_inc(s_mm, 1)
                elif u[0] == "T":
                    q = u[1]
                    eng.wait_ge(exp_ok, g * NTR + q + 1)
                    if some(n := g * NTR + q):
                        eng.wait_ge(pt_sb, n)
                    if q == 0:
                        if some(n := g * DC):
                            eng.wait_ge(x1T_lo_ok, n)
                    for c in range(TR):
                        last = eng.transpose(bank_t[:, c * N:(c + 1) * N], pr[:, q % 2, c, :], ident[:, :])
                    last.then_inc(pt_mm, 1)
                elif u[0] == "V":
                    q = u[1]
                    b, j = divmod(q, HPC)
                    eng.wait_ge(pt_sb, g * NTR + q + 1)
                    eng.wait_ge(v_sb, g * GB + b + 1)
                    if j == 0:
                        if some(n := g * GB + b):
                            eng.wait_ge(att_ok, n)
                    for c in range(TR):
                        hh = c * HPC + j
                        last = eng.matmul(bank_o[:, hh * VW:(hh + 1) * VW], prT[:, q % 2, c, :], v[:, b, hh, :],
                                          start=True, stop=True)
                    last.then_inc(o_mm, 1)
                elif u[0] == "D":
                    c = u[1]
                    if c == 0:
                        eng.wait_ge(pt_sb, (g + 1) * NTR)
                        eng.wait_ge(v_sb, (g + 1) * GB)
                    if c == 2:
                        eng.wait_ge(x1T_lo_ok, g * DC + 1)
                    for b in range(GB):
                        eng.wait_ge(x1_ok, g * GB + b + 1)
                        last = eng.transpose(d_banks[c][:, b * N:(b + 1) * N], xn[:, b, c * P:(c + 1) * P], ident[:, :])
                    last.then_inc(x1T_mm, 1)
                elif u[0] == "N":
                    l, k = u[1], u[2]
                    side, m = divmod(k, DC)
                    x_hi, x_lo = (x1T_hi, x1T_lo) if l == 0 else (h1T_hi, h1T_lo)
                    if k == 0:
                        if l == 0:
                            eng.wait_ge(x1T_lo_ok, (h + 1) * DC)
                        else:
                            eng.wait_ge(h1_lo_ok, (h + 1) * DC)
                        if some(n := h * (GB * L) + GB * l):
                            eng.wait_ge(hl_sb, n)
                    else:
                        if some(n := h * (2 * DC * L) + 2 * DC * l + k):
                            eng.wait_ge(n_sb, n)
                    if isinstance(h, int) and h == 0:
                        eng.wait_ge(w1_lo_done, 3 * L)
                    cols = slice(m * P, (m + 1) * P)
                    split_product(bank_p1[:, :],
                                  lambda c: w1_hi[:, l, side, c, cols], lambda c: w1_lo[:, l, side, c, cols],
                                  lambda c: x_hi[:, c, :], lambda c: x_lo[:, c, :]).then_inc(n_mm, 1)
                elif u[0] == "H":
                    l, b = u[1], u[2]
                    x_hi, x_lo = (x1T_hi, x1T_lo) if l == 0 else (h1T_hi, h1T_lo)
                    if b == 0:
                        eng.wait_ge(n_sb, h * (2 * DC * L) + 2 * DC * (l + 1))
                    else:
                        if some(n := h * (GB * L) + GB * l + b):
                            eng.wait_ge(hl_sb, n)
                    rows = slice(b * N, (b + 1) * N)
                    split_product(bank_p1[:, 0:D],
                                  lambda c: x_hi[:, c, rows], lambda c: x_lo[:, c, rows],
                                  lambda c: w1_hi[:, l, 2, c, :], lambda c: w1_lo[:, l, 2, c, :]).then_inc(hl_mm, 1)
                elif u[0] == "U":
                    l, p = u[1], u[2]
                    eng.wait_ge(n_sb, h * (2 * DC * L) + 2 * DC * (l + 1))
                    if l == 0:
                        eng.wait_ge(hT0_ok, h + 1)
                    else:
                        eng.wait_ge(h1_ok, (h + 1) * DC)
                    if some(n := h * (2 * L) + 2 * l + p):
                        eng.wait_ge(u_sb, n)
                    for b in (2 * p, 2 * p + 1):
                        for c in range(DC):
                            last = eng.matmul(bank_u[:, (b % 2) * 2 * N:(b % 2 + 1) * 2 * N],
                                              hT[:, c, b * N:(b + 1) * N], nT[:, c, :, b * N:(b + 1) * N],
                                              start=(c == 0), stop=(c == DC - 1))
                    last.then_inc(u_mm, 1)
                elif u[0] == "C":
                    l, b = u[1], u[2]
                    eng.wait_ge(e_ok, h * (2 * L) + 2 * l + b // 2 + 1)
                    eng.wait_ge(hl_sb, h * (GB * L) + GB * l + b + 1)
                    if some(n := h * (GB * L) + GB * l + b):
                        eng.wait_ge(c_sb, n)
                    if l == 1 and b == 0:
                        eng.wait_ge(h1_ok, (h + 1) * DC)
                    eng.matmul(bank_c[:, 0:D + 1], uc[:, b, :], hl[:, b, :], start=True, stop=True).then_inc(c_mm, 1)
                elif u[0] == "W":
                    c = u[1]
                    if c == 0:
                        eng.wait_ge(u_sb, h * (2 * L) + 2)
                    elif c == 1:
                        eng.wait_ge(c_sb, h * (GB * L) + GB)
                    else:
                        eng.wait_ge(h1_ok, h * DC + 1)
                    for b in range(GB):
                        eng.wait_ge(y_ok, h * GB + b + 1)
                        last = eng.transpose(w_banks[c][:, b * N:(b + 1) * N], cs[:, b, c * P:(c + 1) * P], ident[:, :])
                    last.then_inc(yT_mm, 1)

            eng.wait_ge(ld_w0, 7 * 16)
            eng.wait_ge(const_done, 5)
            over_iterations(eng, unit)


_OUT = ("out_dram", (G, P, GB, D))


def kernel(**inputs):
    import concourse.bacc as _bacc
    from concourse import mybir as _mybir
    from concourse.bass_utils import run_bass_kernel_spmd as _run

    a = {k: np.ascontiguousarray(x) for k, x in inputs.items()}
    x, adj = a["x"], a["adj"]
    grouped = x.reshape(G, GB, N, D)
    pairs = adj.reshape(G, GB, N, N)

    def columns(b):
        return b.reshape(DC, P).T

    arrays = {
        "xT_in": grouped.reshape(G, T, DC, P).transpose(0, 3, 2, 1),
        "xn_in": grouped.transpose(0, 2, 1, 3),
        "adj_in": pairs.transpose(0, 2, 1, 3),
        "adjT_in": pairs.transpose(0, 3, 1, 2),
        "wq_in": a["L0_gnn_Wq"], "wk_in": a["L0_gnn_Wk"], "wv_in": a["L0_gnn_Wv"],
        "bq_in": columns(a["L0_gnn_bq"]), "bk_in": columns(a["L0_gnn_bk"]), "bv_in": a["L0_gnn_bv"],
        "beta_in": a["L0_gnn_beta"].reshape(1),
        "wl_in": a["L1_gnn_W_left"], "wr_in": a["L1_gnn_W_right"],
        "wlin_in": a["L1_gnn_W_lin"].transpose(0, 2, 1),
        "blin_in": a["L1_gnn_b_lin"],
        "lna_col_in": columns(a["L1_gnn_ln_a"][0]), "lnb_col_in": columns(a["L1_gnn_ln_b"][0]),
        "lna_in": a["L1_gnn_ln_a"][1], "lnb_in": a["L1_gnn_ln_b"][1],
    }
    arrays = {k: np.ascontiguousarray(w) for k, w in arrays.items()}
    nc = _bacc.Bacc("TRN2", target_bir_lowering=False, num_devices=1)
    args = [nc.dram_tensor(k, w.shape, _mybir.dt.from_np(w.dtype), kind="ExternalInput").ap() for k, w in arrays.items()]
    args.append(nc.dram_tensor(_OUT[0], _OUT[1], F32, kind="ExternalOutput").ap())
    graph_blocks(nc, *args)
    r = _run(nc, [arrays], core_ids=[0])
    got = r.results[0][_OUT[0]]
    return np.ascontiguousarray(got.transpose(0, 2, 1, 3)).reshape(NB, N, D)
```

```python
from contextlib import ExitStack

import numpy as np

import concourse.bass as bass
from concourse import mybir

F32 = mybir.dt.float32
F32R = mybir.dt.float32r
ALU = mybir.AluOpType
ACT = mybir.ActivationFunctionType
AX = mybir.AxisListType

P = 128
NB, N, D = 64, 128, 384
H = 12
HD = D // H
GB = 4
G = NB // GB
T = GB * N
DC = D // P
HPC = P // HD
NQ = GB * DC
L = 2
VW = HD + 1
MASKED = -9000000000000000.0
LN_EPS, L1_EPS, SUM_EPS = 1e-5, 1e-3, 1e-10


def attention_step(q):
    units = []
    if q < NQ:
        units.append(("S", q))
    if q in (DC + 1, 2 * DC + 1):
        units.append(("K", q // DC + 1))
    if 0 <= q - 3 < NQ:
        units.append(("T", q - 3))
    if 0 <= q - 4 < NQ:
        units.append(("V", q - 4))
    return [(0, u) for u in units]


def turn():
    beside = {
        1: [("N", 1, 0)], 2: [("N", 1, 1)], 3: [("N", 1, 2)], 4: [("N", 1, 3)], 5: [("N", 1, 4)], 6: [("N", 1, 5)],
        7: [("U", 1, 0)], 8: [("H", 1, 0)], 9: [("E", 1, 0), ("U", 1, 1)], 10: [("H", 1, 1)],
        11: [("E", 1, 1), ("H", 1, 2)], 12: [("H", 1, 3)], 13: [("C", 1, 0)], 14: [("C", 1, 1)],
    }
    units = []
    for q in range(NQ + 4):
        units += attention_step(q) + [(-1, u) for u in beside.get(q, [])]
    units += [(0, ("X", 0)), (-1, ("C", 1, 2)), (1, ("A", 0)), (-1, ("C", 1, 3)), (1, ("A", 1)), (-1, ("F", 0)),
              (0, ("X", 1)), (0, ("D", 0)), (0, ("D", 1)), (0, ("D", 2)), (-1, ("F", 1)), (1, ("A", 2)),
              (0, ("R", 0))]
    for k in range(2 * DC):
        units += [(0, ("N", 0, k)), (-1, ("F", k + 2))]
    units += [(0, ("R", 1)), (0, ("H", 0, 0)), (0, ("H", 0, 1)), (0, ("U", 0, 0)), (0, ("H", 0, 2)),
              (0, ("E", 0, 0)), (0, ("U", 0, 1)), (0, ("H", 0, 3)), (1, ("A", 3)),
              (0, ("C", 0, 0)), (0, ("E", 0, 1)), (0, ("C", 0, 1)), (1, ("A", 4)), (0, ("C", 0, 2)), (0, ("C", 0, 3)),
              (1, ("A", 5)), (0, ("Y", 0)), (1, ("B", 0)), (0, ("Y", 1)), (1, ("B", 1)), (0, ("Y", 2)),
              (1, ("B", 2)), (1, ("K", 0)), (0, ("W", 0)), (0, ("W", 1)), (0, ("W", 2)), (1, ("B", 3)), (1, ("K", 1))]
    return units


def graph_blocks(nc, xT_d, xn_d, adj_d, adjT_d, wq_d, wk_d, wv_d, bq_d, bk_d, bv_d, beta_d,
                 wl_d, wr_d, wlin_d, blin_d, lna_col_d, lnb_col_d, lna_d, lnb_d, out_d):
    with ExitStack() as ctx:
        def sb(name, shape, dt=F32):
            return ctx.enter_context(nc.sbuf_tensor(name, shape, dt))

        def bank(name):
            return ctx.enter_context(nc.psum_tensor(name, [P, 512], F32))

        def sem(name):
            return ctx.enter_context(nc.semaphore(name))

        wqk = sb("wqk", [P, 2, DC, D])
        wv = sb("wv", [P, DC, D])
        w1_hi = sb("w1_hi", [P, L, 3, DC, D], F32R)
        w1_lo = sb("w1_lo", [P, L, 3, DC, D], F32R)
        bqk = sb("bqk", [P, 2, DC])
        bv_b = sb("bv_b", [P, D])
        blin_b = sb("blin_b", [P, L, D])
        lna_b = sb("lna_b", [P, D])
        lnb_b = sb("lnb_b", [P, D])
        lna_c = sb("lna_c", [P, DC])
        lnb_c = sb("lnb_c", [P, DC])
        beta = sb("beta", [P, 1])
        ident = sb("ident", [P, P])
        half = sb("half", [P, 2, GB])

        xT = sb("xT", [P, DC, T])
        xn = sb("xn", [P, GB, D])
        adj = sb("adj", [P, GB, N])
        bias = sb("bias", [P, GB, N])
        qkT = sb("qkT", [P, 2, DC, T])
        v = sb("v", [P, GB, H, VW])
        kz = sb("kz", [P, 2, DC, HPC, N])
        sm = sb("sm", [P, 2, HPC, N])
        nmax = sb("nmax", [P, 2, HPC])
        pr = sb("pr", [P, 3, HPC, N])
        prT = sb("prT", [P, 2, HPC, N])
        rden = sb("rden", [P, 2, H])
        att = sb("att", [P, 2, D])
        st0 = sb("st0", [P, GB, 6])
        mv0 = sb("mv0", [P, GB, 2])
        ve0 = sb("ve0", [P, GB])
        rs0 = sb("rs0", [P, GB])

        hT_hi = sb("hT_hi", [P, DC, T], F32R)
        hT_lo = sb("hT_lo", [P, DC, T], F32R)
        hT = sb("hT", [P, DC, T])
        x1 = sb("x1", [P, GB, D])
        adj1 = sb("adj1", [P, 2, GB, N])
        tri = sb("tri", [P, GB, 2, N])
        nT = sb("nT", [P, DC, 2, T])
        hl = sb("hl", [P, GB, D + 1])
        uw = sb("uw", [P, 2, 2, N])
        uc = sb("uc", [P, GB, N])
        cs = sb("cs", [P, GB, D + 1])
        st1 = sb("st1", [P, GB, 6])
        mv1 = sb("mv1", [P, GB, 2])
        sc = sb("sc", [P, 5, GB])
        stf = sb("stf", [P, GB, 6])
        mvf = sb("mvf", [P, GB, 2])
        rsf = sb("rsf", [P, 2, GB])

        bank_p0, bank_s0, bank_s1, bank_t, bank_o, bank_p1, bank_u, bank_c = (
            bank(n) for n in ("bank_p0", "bank_s0", "bank_s1", "bank_t", "bank_o", "bank_p1", "bank_u", "bank_c"))
        bank_s = [bank_s0, bank_s1]
        d_banks = [bank_t, bank_o, bank_s0]
        w_banks = [bank_u, bank_c, bank_p1]
        c_banks = [bank_c, bank_p1]
        proj_banks = [bank_p0, bank_s1]

        def nh_bank(l, k):
            return (bank_p1, bank_p0 if l else bank_c)[k % 2]

        ld_w0 = sem("ld_w0")
        ld_w1 = sem("ld_w1")
        ld_w1s = [sem(f"ld_w1s{i}") for i in range(3 * L)]
        w1_hi_done = sem("w1_hi_done")
        w1_lo_done = sem("w1_lo_done")
        const_done = sem("const_done")
        ident_zero = sem("ident_zero")
        ld_xT = sem("ld_xT")
        ld_xn = sem("ld_xn")
        ld_adj = sem("ld_adj")
        ld_adj1 = sem("ld_adj1")
        st_out = sem("st_out")
        qk_mm = sem("qk_mm")
        qk_sb = sem("qk_sb")
        kz_zero = sem("kz_zero")
        kz_ok = sem("kz_ok")
        v_mm = sem("v_mm")
        v_sb = sem("v_sb")
        pen_ok = sem("pen_ok")
        bias_ok = sem("bias_ok")
        s_mm = sem("s_mm")
        s_sb = sem("s_sb")
        nmax_ok = sem("nmax_ok")
        exp_ok = sem("exp_ok")
        pt_mm = sem("pt_mm")
        pt_sb = sem("pt_sb")
        o_mm = sem("o_mm")
        rden_ok = sem("rden_ok")
        att_ok = sem("att_ok")
        res0_ok = sem("res0_ok")
        st0_ok = sem("st0_ok")
        mv0_ok = sem("mv0_ok")
        ve0_ok = sem("ve0_ok")
        rs0_ok = sem("rs0_ok")
        x1_ok = sem("x1_ok")
        x1T_mm = sem("x1T_mm")
        x1T_hi_ok = sem("x1T_hi_ok")
        x1T_lo_ok = sem("x1T_lo_ok")
        x1_kept = sem("x1_kept")
        hT0_ok = sem("hT0_ok")
        tri_ok = sem("tri_ok")
        n_mm = sem("n_mm")
        n_sb = sem("n_sb")
        hl_mm = sem("hl_mm")
        hl_sb = sem("hl_sb")
        u_mm = sem("u_mm")
        u_sb = sem("u_sb")
        ut_ok = sem("ut_ok")
        ue_ok = sem("ue_ok")
        e_ok = sem("e_ok")
        c_mm = sem("c_mm")
        c_sb = sem("c_sb")
        st1_ok = sem("st1_ok")
        mv1_ok = sem("mv1_ok")
        sc_ok = sem("sc_ok")
        sd_ok = sem("sd_ok")
        y_ok = sem("y_ok")
        yT_mm = sem("yT_mm")
        h1_ok = sem("h1_ok")
        h1_hi_ok = sem("h1_hi_ok")
        h1_lo_ok = sem("h1_lo_ok")
        fa_ok = sem("fa_ok")
        fb_ok = sem("fb_ok")
        res1_ok = sem("res1_ok")
        stf_ok = sem("stf_ok")
        mvf_ok = sem("mvf_ok")
        vef_ok = sem("vef_ok")
        rsf_ok = sem("rsf_ok")
        carrier = sem("carrier")
        out_ok = sem("out_ok")

        def some(value):
            return not isinstance(value, int) or value > 0

        def alone(eng):
            eng.sem_inc(carrier, 1)

        block = ctx.enter_context(nc.Block())

        stage = [nT[:, :, 0, 0:D], nT[:, :, 1, 0:D], hT[:, :, 0:D]]
        w1_src = [w[l].rearrange("(c p) n -> p c n", p=P) for l in range(L) for w in (wl_d, wr_d, wlin_d)]

        def over_turns(eng, unit):
            for i in (-1, 0):
                for shift, u in turn():
                    if i + shift >= 0:
                        unit(u, i + shift)
            with eng.Fori(1, G - 1) as i:
                for shift, u in turn():
                    unit(u, i + shift)
            for i in (G - 1, G):
                for shift, u in turn():
                    if i + shift < G:
                        unit(u, i + shift)

        @block.sync
        def _(eng):
            def load_xT(g):
                if some(n := g * GB):
                    eng.wait_ge(v_mm, n)
                    alone(eng)
                eng.dma_start(xT[:, :, :], xT_d[g]).then_inc(ld_xT, 16)

            def load_adj(g):
                if some(n := g):
                    eng.wait_ge(bias_ok, n)
                    alone(eng)
                eng.dma_start(adj[:, :, :], adj_d[g]).then_inc(ld_adj, 16)

            def load_xn(g):
                if some(n := g):
                    eng.wait_ge(x1_kept, n)
                    alone(eng)
                    eng.wait_ge(x1T_mm, g * DC)
                    alone(eng)
                eng.dma_start(xn[:, :, :], xn_d[g]).then_inc(ld_xn, 16)

            def load_adj1(h):
                if some(n := h * (2 * L)):
                    eng.wait_ge(e_ok, n)
                    alone(eng)
                    eng.wait_ge(tri_ok, h * 2)
                    alone(eng)
                eng.dma_start(adj1[:, 0, :, :], adj_d[h]).then_inc(ld_adj1, 16)
                eng.dma_start(adj1[:, 1, :, :], adjT_d[h]).then_inc(ld_adj1, 16)

            def store(h):
                eng.wait_ge(out_ok, (h + 1) * GB)
                alone(eng)
                eng.dma_start(out_d[h], cs[:, :, 0:D]).then_inc(st_out, 16)

            eng.dma_start(xT[:, :, :], xT_d[0]).then_inc(ld_xT, 16)
            for i, w in enumerate((wq_d, wk_d)):
                eng.dma_start(wqk[:, i, :, :], w.rearrange("(c p) n -> p c n", p=P)).then_inc(ld_w0, 16)
            eng.dma_start(bqk[:, 0, :], bq_d).then_inc(ld_w0, 16)
            eng.dma_start(bqk[:, 1, :], bk_d).then_inc(ld_w0, 16)
            eng.dma_start(wv[:, :, :], wv_d.rearrange("(c p) n -> p c n", p=P)).then_inc(ld_w0, 16)
            eng.dma_start(bv_b[:, :], bv_d.partition_broadcast(P)).then_inc(ld_w0, 16)
            eng.dma_start(beta[:, :], beta_d.partition_broadcast(P)).then_inc(ld_w0, 16)
            eng.dma_start(adj[:, :, :], adj_d[0]).then_inc(ld_adj, 16)
            for i in range(3):
                eng.dma_start(stage[i], w1_src[i]).then_inc(ld_w1s[i], 16)
            load_xn(0)
            for l in range(L):
                eng.dma_start(blin_b[:, l, :], blin_d[l].partition_broadcast(P)).then_inc(ld_w1, 16)
            eng.dma_start(lna_b[:, :], lna_d.partition_broadcast(P)).then_inc(ld_w1, 16)
            eng.dma_start(lnb_b[:, :], lnb_d.partition_broadcast(P)).then_inc(ld_w1, 16)
            eng.dma_start(lna_c[:, :], lna_col_d).then_inc(ld_w1, 16)
            eng.dma_start(lnb_c[:, :], lnb_col_d).then_inc(ld_w1, 16)
            for i in range(3, 3 * L):
                eng.wait_ge(w1_lo_done, i - 2)
                eng.dma_start(stage[i - 3], w1_src[i]).then_inc(ld_w1s[i], 16)
            load_xT(1)
            load_adj(1)
            load_adj1(0)
            with eng.Fori(1, G - 1) as i:
                load_xn(i)
                load_xT(i + 1)
                load_adj(i + 1)
                load_adj1(i)
                store(i - 1)
            load_xn(G - 1)
            load_adj1(G - 1)
            store(G - 2)
            store(G - 1)
            eng.wait_ge(st_out, 16 * G)

        @block.gpsimd
        def _(eng):
            eng.memset(ident[:, :], 0.0).then_inc(ident_zero, 1)
            eng.memset(half[:, 0, :], -0.5).then_inc(const_done, 1)
            eng.memset(half[:, 1, :], 0.5).then_inc(const_done, 1)
            eng.memset(v[:, :, :, HD:VW], 1.0).then_inc(const_done, 1)
            eng.memset(hl[:, :, D:D + 1], 1.0).then_inc(const_done, 1)
            eng.wait_ge(ident_zero, 1)
            eng.affine_select(out=ident[:, :], in_=ident[:, :], compare_op=ALU.not_equal, fill=1.0,
                              base=0, pattern=[[-1, P]], channel_multiplier=1).then_inc(const_done, 1)
            eng.memset(kz[:, :, :, :, :], 0.0).then_inc(kz_zero, 1)
            for i in range(3 * L):
                eng.wait_ge(w1_hi_done, i + 1)
                eng.tensor_tensor(w1_lo[:, i // 3, i % 3, :, :], stage[i % 3],
                                  w1_hi[:, i // 3, i % 3, :, :].bitcast(F32), ALU.subtract).then_inc(w1_lo_done, 1)

            def unit(u, g):
                h = g
                if u[0] == "V" and u[1] % DC == DC - 1:
                    b = u[1] // DC
                    eng.wait_ge(att_ok, g * GB + b + 1)
                    eng.wait_ge(ld_xn, (g + 1) * 16)
                    eng.tensor_tensor(xn[:, b, :], xn[:, b, :], att[:, b % 2, :], ALU.add).then_inc(res0_ok, 1)
                elif u[0] == "X" and u[1] == 0:
                    eng.wait_ge(ve0_ok, g + 1)
                    if some(n := g * GB):
                        eng.wait_ge(x1_ok, n)
                    eng.tensor_tensor(rs0[:, :], ve0[:, :], half[:, 0, :], ALU.pow).then_inc(rs0_ok, 1)
                elif u == ("R", 0):
                    eng.wait_ge(x1T_lo_ok, (h + 1) * DC)
                    if some(n := h * (2 * L)):
                        eng.wait_ge(u_mm, n)
                    eng.tensor_tensor(hT[:, :, :], hT_hi[:, :, :].bitcast(F32), hT_lo[:, :, :].bitcast(F32),
                                      ALU.add).then_inc(hT0_ok, 1)
                    eng.wait_ge(ld_adj1, (h + 1) * 32)
                    if some(n := h * (2 * L)):
                        eng.wait_ge(u_sb, n)
                    alone(eng)
                    eng.affine_select(out=tri[:, :, 0, :], in_=adj1[:, 1, :, :], compare_op=ALU.is_ge, fill=0.0,
                                      base=0, pattern=[[0, GB], [-1, N]], channel_multiplier=1).then_inc(tri_ok, 1)
                    eng.affine_select(out=tri[:, :, 1, :], in_=adj1[:, 0, :, :], compare_op=ALU.is_gt, fill=0.0,
                                      base=0, pattern=[[0, GB], [1, N]], channel_multiplier=-1).then_inc(tri_ok, 1)
                elif u == ("R", 1):
                    if some(n := h * GB):
                        eng.wait_ge(res1_ok, n)
                    eng.wait_ge(x1_ok, (h + 1) * GB)
                    alone(eng)
                    eng.tensor_copy(x1[:, :, :], xn[:, :, :]).then_inc(x1_kept, 1)
                elif u[0] == "W":
                    c = u[1]
                    eng.wait_ge(h1_hi_ok, h * DC + c + 1)
                    eng.tensor_tensor(hT_lo[:, c, :], hT[:, c, :], hT_hi[:, c, :].bitcast(F32),
                                      ALU.subtract).then_inc(h1_lo_ok, 1)
                elif u == ("Y", 0):
                    sd(0, h)
                elif u == ("F", 0):
                    sd(L - 1, h)
                elif u == ("F", 6):
                    eng.wait_ge(vef_ok, h + 1)
                    eng.tensor_tensor(rsf[:, 1, :], rsf[:, 0, :], half[:, 0, :], ALU.pow).then_inc(rsf_ok, 1)

            def sd(l, h):
                eng.wait_ge(sc_ok, h * (4 * L) + 4 * l + 1)
                eng.tensor_tensor(sc[:, 1, :], sc[:, 0, :], half[:, 1, :], ALU.pow).then_inc(sd_ok, 1)

            eng.wait_ge(const_done, 5)
            over_turns(eng, unit)

        @block.scalar
        def _(eng):
            for i in range(3 * L):
                eng.wait_ge(ld_w1s[i], 16)
                eng.activation(w1_hi[:, i // 3, i % 3, :, :], stage[i % 3], ACT.Copy).then_inc(w1_hi_done, 1)
                if i == 2:
                    eng.wait_ge(ld_w0, 7 * 16)

            def unit(u, g):
                h = g
                if u[0] == "A":
                    i, c = divmod(u[1], DC)
                    eng.wait_ge(qk_mm, g * (2 * DC) + u[1] + 1)
                    if some(n := g * NQ):
                        eng.wait_ge(s_mm, n)
                    eng.activation(qkT[:, i, c, :], proj_banks[u[1] % 2][:, :], ACT.Identity,
                                   bias=bqk[:, i, c:c + 1]).then_inc(qk_sb, 1)
                elif u[0] == "S":
                    q = u[1]
                    eng.wait_ge(nmax_ok, g * NQ + q + 1)
                    if some(n := g * NQ + q - 2):
                        eng.wait_ge(pt_mm, n)
                    for j in range(HPC):
                        last = eng.activation(pr[:, q % 3, j, :], sm[:, q % 2, j, :], ACT.Exp,
                                              bias=nmax[:, q % 2, j:j + 1])
                    last.then_inc(exp_ok, 1)
                elif u[0] == "T":
                    q = u[1]
                    eng.wait_ge(pt_mm, g * NQ + q + 1)
                    if some(n := g * NQ + q - 1):
                        eng.wait_ge(o_mm, n)
                    eng.activation(prT[:, q % 2, :, :], bank_t[:, :], ACT.Copy).then_inc(pt_sb, 1)
                elif u[0] == "D":
                    c = u[1]
                    eng.wait_ge(x1T_mm, g * DC + c + 1)
                    if some(n := g * (L * GB)):
                        eng.wait_ge(hl_mm, n)
                    eng.activation(hT_hi[:, c, :], d_banks[c][:, :], ACT.Copy).then_inc(x1T_hi_ok, 1)
                elif u[0] == "N":
                    l, k = u[1], u[2]
                    side, c = divmod(k, DC)
                    eng.wait_ge(n_mm, h * (2 * DC * L) + 2 * DC * l + k + 1)
                    if some(n := h * (2 * L) + 2 * l):
                        eng.wait_ge(u_mm, n)
                    eng.activation(nT[:, c, side, :], nh_bank(l, k)[:, :], ACT.Copy).then_inc(n_sb, 1)
                elif u[0] == "E":
                    l, p = u[1], u[2]
                    eng.wait_ge(ut_ok, h * (2 * L) + 2 * l + p + 1)
                    eng.activation(uc[:, 2 * p:2 * p + 2, :], uc[:, 2 * p:2 * p + 2, :], ACT.Exp,
                                   scale=float(1.0 / np.sqrt(D))).then_inc(ue_ok, 1)
                elif u[0] == "C":
                    l, b = u[1], u[2]
                    eng.wait_ge(c_mm, h * (GB * L) + GB * l + b + 1)
                    if l == 0:
                        if some(n := h * 16):
                            eng.wait_ge(st_out, n)
                    else:
                        eng.wait_ge(yT_mm, (h + 1) * DC)
                    eng.activation(cs[:, b, :], c_banks[b % 2][:, 0:D + 1], ACT.Copy).then_inc(c_sb, 1)
                elif u[0] == "W":
                    c = u[1]
                    eng.wait_ge(yT_mm, h * DC + c + 1)
                    eng.wait_ge(u_mm, h * (2 * L) + 2)
                    eng.activation(hT[:, c, :], w_banks[c][:, :], ACT.Relu, bias=lnb_c[:, c:c + 1],
                                   scale=lna_c[:, c:c + 1]).then_inc(h1_ok, 1)

            over_turns(eng, unit)

        @block.vector
        def _(eng):
            def make_bias(g):
                eng.wait_ge(ld_adj, (g + 1) * 16)
                if some(n := g * NQ):
                    eng.wait_ge(s_sb, n)
                eng.tensor_scalar(bias[:, :, :], adj[:, :, :], 0.0, MASKED, ALU.is_le, ALU.mult).then_inc(pen_ok, 1)
                eng.wait_ge(pen_ok, g + 1)
                eng.scalar_tensor_tensor(out=bias[:, :, :], in0=adj[:, :, :], scalar=beta[:, 0:1], in1=bias[:, :, :],
                                         op0=ALU.mult, op1=ALU.add).then_inc(bias_ok, 1)

            def unit(u, g):
                h = g
                if u[0] == "A" and u[1] == 2:
                    make_bias(g)
                elif u[0] == "K":
                    b = u[1]
                    eng.wait_ge(qk_sb, (g + 1) * (2 * DC))
                    if some(n := g * NQ + DC * (b - 1)):
                        eng.wait_ge(s_mm, n)
                    for j in range(HPC):
                        rows = slice(j * HD, (j + 1) * HD)
                        eng.tensor_copy(kz[rows, b % 2, :, j, :], qkT[rows, 1, :, b * N:(b + 1) * N]).then_inc(kz_ok, 1)
                elif u[0] == "B":
                    b = u[1]
                    eng.wait_ge(v_mm, g * GB + b + 1)
                    if some(n := g * NQ + DC * (b + 1) - NQ):
                        eng.wait_ge(o_mm, n)
                    eng.tensor_tensor(v[:, b, :, 0:HD],
                                      proj_banks[b % 2][:, 0:D].rearrange("p (h d) -> p h d", h=H),
                                      bv_b[:, :].rearrange("p (h d) -> p h d", h=H), ALU.add).then_inc(v_sb, 1)
                elif u[0] == "S":
                    q = u[1]
                    b = q // DC
                    eng.wait_ge(s_mm, g * NQ + q + 1)
                    if some(n := g * NQ + q - 1):
                        eng.wait_ge(exp_ok, n)
                    eng.wait_ge(bias_ok, g + 1)
                    eng.scalar_tensor_tensor(
                        out=sm[:, q % 2, :, :], in0=bank_s[q % 2][:, :].rearrange("p (t n) -> p t n", t=HPC),
                        scalar=float(1.0 / np.sqrt(HD)),
                        in1=bias[:, b:b + 1, :].to_broadcast([P, HPC, N]), op0=ALU.mult, op1=ALU.add).then_inc(s_sb, 1)
                    eng.wait_ge(s_sb, g * NQ + q + 1)
                    eng.tensor_reduce(nmax[:, q % 2, :], sm[:, q % 2, :, :], AX.X, ALU.max,
                                      negate=True).then_inc(nmax_ok, 1)
                elif u[0] == "V":
                    q = u[1]
                    b = q // DC
                    if q % DC == DC - 1:
                        o = bank_o[:, 0:H * VW].rearrange("p (h d) -> p h d", h=H)
                        eng.wait_ge(o_mm, g * NQ + q + 1)
                        eng.reciprocal(rden[:, b % 2, :], o[:, :, HD]).then_inc(rden_ok, 1)
                        eng.wait_ge(rden_ok, g * GB + b + 1)
                        if some(n := g * GB + b - 1):
                            eng.wait_ge(res0_ok, n)
                        eng.tensor_tensor(att[:, b % 2, :].rearrange("p (h d) -> p h d", h=H), o[:, :, 0:HD],
                                          rden[:, b % 2, :].unsqueeze(2).to_broadcast([P, H, HD]),
                                          ALU.mult).then_inc(att_ok, 1)
                    if b > 0 and q % DC == 1:
                        stats0(g, b - 1)
                elif u == ("X", 0):
                    stats0(g, GB - 1)
                    for b in range(GB):
                        eng.wait_ge(st0_ok, g * GB + b + 1)
                        alone(eng)
                        last = eng.bn_aggr(mv0[:, b, :], st0[:, b, :])
                    last.then_inc(mv0_ok, 1)
                    eng.wait_ge(mv0_ok, g + 1)
                    eng.tensor_scalar(ve0[:, :], mv0[:, :, 1], LN_EPS, None, ALU.add).then_inc(ve0_ok, 1)
                elif u == ("X", 1):
                    eng.wait_ge(rs0_ok, g + 1)
                    for b in range(GB):
                        eng.tensor_scalar(xn[:, b, :], xn[:, b, :], mv0[:, b, 0:1], rs0[:, b:b + 1],
                                          ALU.subtract, ALU.mult).then_inc(x1_ok, 1)
                elif u[0] == "D":
                    c = u[1]
                    eng.wait_ge(x1T_hi_ok, g * DC + c + 1)
                    eng.tensor_tensor(hT_lo[:, c, :], d_banks[c][:, :], hT_hi[:, c, :].bitcast(F32),
                                      ALU.subtract).then_inc(x1T_lo_ok, 1)
                elif u[0] == "H":
                    l, b = u[1], u[2]
                    eng.wait_ge(hl_mm, h * (GB * L) + GB * l + b + 1)
                    if some(n := h * (GB * L) + GB * (l - 1) + b + 1):
                        eng.wait_ge(c_mm, n)
                    eng.tensor_tensor(hl[:, b, 0:D], nh_bank(l, b)[:, 0:D], blin_b[:, l, :], ALU.add).then_inc(hl_sb, 1)
                elif u[0] == "U":
                    l, p = u[1], u[2]
                    eng.wait_ge(u_mm, h * (2 * L) + 2 * l + p + 1)
                    eng.wait_ge(tri_ok, (h + 1) * 2)
                    if some(n := h * (2 * L) + 2 * l + p):
                        eng.wait_ge(ut_ok, n)
                    eng.tensor_tensor(uw[:, :, :, :], bank_u[:, :].rearrange("p (b s n) -> p b s n", b=2, s=2),
                                      tri[:, 2 * p:2 * p + 2, :, :], ALU.mult).then_inc(u_sb, 1)
                    eng.wait_ge(u_sb, h * (2 * L) + 2 * l + p + 1)
                    if some(n := h * (GB * L) + GB * (l - 1) + 2 * p + 2):
                        eng.wait_ge(c_mm, n)
                    eng.tensor_tensor(uc[:, 2 * p:2 * p + 2, :], uw[:, :, 0, :], uw[:, :, 1, :],
                                      ALU.add).then_inc(ut_ok, 1)
                elif u[0] == "E":
                    l, p = u[1], u[2]
                    eng.wait_ge(ue_ok, h * (2 * L) + 2 * l + p + 1)
                    eng.tensor_tensor(uc[:, 2 * p:2 * p + 2, :], uc[:, 2 * p:2 * p + 2, :],
                                      adj1[:, 1, 2 * p:2 * p + 2, :], ALU.mult).then_inc(e_ok, 1)
                elif u[0] == "C":
                    l, b = u[1], u[2]
                    eng.wait_ge(c_sb, h * (GB * L) + GB * l + b + 1)
                    eng.bn_stats(st1[:, b, :], cs[:, b, 0:D]).then_inc(st1_ok, 1)
                elif u == ("Y", 0):
                    context_stats(0, h)
                elif u == ("Y", 1):
                    context_scale(0, h)
                elif u == ("Y", 2):
                    eng.wait_ge(sc_ok, h * (4 * L) + 4)
                    for b in range(GB):
                        eng.tensor_scalar(cs[:, b, 0:D], cs[:, b, 0:D], mv1[:, b, 0:1], sc[:, 4, b:b + 1],
                                          ALU.subtract, ALU.mult).then_inc(y_ok, 1)
                elif u == ("F", 0):
                    context_stats(L - 1, h)
                elif u == ("F", 1):
                    context_scale(L - 1, h)
                elif u[0] == "F":
                    last_norm(h, u[1] - 2)
                elif u[0] == "W":
                    c = u[1]
                    eng.wait_ge(h1_ok, h * DC + c + 1)
                    eng.wait_ge(hl_mm, h * (L * GB) + GB)
                    eng.tensor_copy(hT_hi[:, c, :], hT[:, c, :]).then_inc(h1_hi_ok, 1)

            def stats0(g, b):
                eng.wait_ge(res0_ok, g * GB + b + 1)
                eng.bn_stats(st0[:, b, :], xn[:, b, :]).then_inc(st0_ok, 1)

            def context_stats(l, h):
                eng.wait_ge(st1_ok, h * (GB * L) + GB * l + GB)
                alone(eng)
                for b in range(GB):
                    last = eng.bn_aggr(mv1[:, b, :], st1[:, b, :])
                last.then_inc(mv1_ok, 1)
                eng.wait_ge(mv1_ok, h * L + l + 1)
                eng.tensor_scalar(sc[:, 0, :], mv1[:, :, 1], float(D) / (D - 1), None, ALU.mult).then_inc(sc_ok, 1)
                eng.tensor_scalar(sc[:, 2, :], cs[:, :, D], SUM_EPS, None, ALU.add).then_inc(sc_ok, 1)

            def context_scale(l, h):
                eng.wait_ge(sc_ok, h * (4 * L) + 4 * l + 2)
                eng.wait_ge(sd_ok, h * L + l + 1)
                eng.scalar_tensor_tensor(out=sc[:, 3, :], in0=sc[:, 2, :], scalar=L1_EPS, in1=sc[:, 1, :],
                                         op0=ALU.mult, op1=ALU.add).then_inc(sc_ok, 1)
                eng.wait_ge(sc_ok, h * (4 * L) + 4 * l + 3)
                eng.reciprocal(sc[:, 4, :], sc[:, 3, :]).then_inc(sc_ok, 1)

            def last_norm(h, b):
                if b < GB:
                    eng.wait_ge(sc_ok, (h + 1) * (4 * L))
                    eng.scalar_tensor_tensor(out=cs[:, b, 0:D], in0=cs[:, b, 0:D], scalar=mv1[:, b, 0:1],
                                             in1=lna_b[:, :], op0=ALU.subtract, op1=ALU.mult).then_inc(fa_ok, 1)
                    eng.wait_ge(fa_ok, h * GB + b + 1)
                    eng.scalar_tensor_tensor(out=cs[:, b, 0:D], in0=cs[:, b, 0:D], scalar=sc[:, 4, b:b + 1],
                                             in1=lnb_b[:, :], op0=ALU.mult, op1=ALU.add).then_inc(fb_ok, 1)
                    eng.wait_ge(fb_ok, h * GB + b + 1)
                    eng.wait_ge(x1_kept, h + 1)
                    eng.scalar_tensor_tensor(out=cs[:, b, 0:D], in0=cs[:, b, 0:D], scalar=0.0,
                                             in1=x1[:, b, :], op0=ALU.max, op1=ALU.add).then_inc(res1_ok, 1)
                    eng.wait_ge(res1_ok, h * GB + b + 1)
                    eng.bn_stats(stf[:, b, :], cs[:, b, 0:D]).then_inc(stf_ok, 1)
                elif b == GB:
                    eng.wait_ge(stf_ok, (h + 1) * GB)
                    alone(eng)
                    for b in range(GB):
                        last = eng.bn_aggr(mvf[:, b, :], stf[:, b, :])
                    last.then_inc(mvf_ok, 1)
                    eng.wait_ge(mvf_ok, h + 1)
                    eng.tensor_scalar(rsf[:, 0, :], mvf[:, :, 1], LN_EPS, None, ALU.add).then_inc(vef_ok, 1)
                else:
                    eng.wait_ge(rsf_ok, h + 1)
                    for b in range(GB):
                        eng.tensor_scalar(cs[:, b, 0:D], cs[:, b, 0:D], mvf[:, b, 0:1], rsf[:, 1, b:b + 1],
                                          ALU.subtract, ALU.mult).then_inc(out_ok, 1)

            eng.wait_ge(ld_w0, 7 * 16)
            eng.wait_ge(ld_w1, 6 * 16)
            eng.wait_ge(kz_zero, 1)
            over_turns(eng, unit)

        @block.tensor
        def _(eng):
            def split_product(out, w_hi, w_lo, x_hi, x_lo):
                for c in range(DC):
                    for n, (a, b) in enumerate(((w_hi, x_hi), (w_hi, x_lo), (w_lo, x_hi))):
                        last = eng.matmul(out, a(c), b(c), start=(c == 0 and n == 0), stop=(c == DC - 1 and n == 2))
                return last

            def unit(u, g):
                h = g
                if u[0] == "A":
                    i, m = divmod(u[1], DC)
                    if u[1] == 0:
                        eng.wait_ge(ld_xT, (g + 1) * 16)
                        if some(n := g * GB):
                            eng.wait_ge(v_sb, n)
                        if some(n := g * NQ):
                            eng.wait_ge(s_sb, n)
                    elif u[1] > 1:
                        eng.wait_ge(qk_sb, g * (2 * DC) + u[1] - 1)
                    for c in range(DC):
                        last = eng.matmul(proj_banks[u[1] % 2][:, :], wqk[:, i, c, m * P:(m + 1) * P], xT[:, c, :],
                                          start=(c == 0), stop=(c == DC - 1))
                    last.then_inc(qk_mm, 1)
                elif u[0] == "B":
                    b = u[1]
                    if b < 2:
                        eng.wait_ge(qk_sb, (g + 1) * (2 * DC) - 1 + b)
                    else:
                        eng.wait_ge(v_sb, g * GB + b - 1)
                    for c in range(DC):
                        last = eng.matmul(proj_banks[b % 2][:, 0:D], xT[:, c, b * N:(b + 1) * N], wv[:, c, :],
                                          start=(c == 0), stop=(c == DC - 1))
                    last.then_inc(v_mm, 1)
                elif u[0] == "S":
                    q = u[1]
                    b, c = divmod(q, DC)
                    eng.wait_ge(kz_ok, g * (GB * HPC) + HPC * (b + 1))
                    if some(n := g * NQ + q - 1):
                        eng.wait_ge(s_sb, n)
                    if q == 0:
                        if some(n := g * DC):
                            eng.wait_ge(x1T_lo_ok, n)
                        eng.wait_ge(v_sb, (g + 1) * GB)
                    eng.matmul(bank_s[q % 2][:, :], qkT[:, 0, c, b * N:(b + 1) * N], kz[:, b % 2, c, :, :],
                               start=True, stop=True).then_inc(s_mm, 1)
                elif u[0] == "T":
                    q = u[1]
                    eng.wait_ge(exp_ok, g * NQ + q + 1)
                    if some(n := g * NQ + q):
                        eng.wait_ge(pt_sb, n)
                    for c in range(HPC):
                        last = eng.transpose(bank_t[:, c * N:(c + 1) * N], pr[:, q % 3, c, :], ident[:, :])
                    last.then_inc(pt_mm, 1)
                elif u[0] == "V":
                    q = u[1]
                    b, c = divmod(q, DC)
                    eng.wait_ge(pt_sb, g * NQ + q + 1)
                    eng.wait_ge(v_sb, g * GB + b + 1)
                    if c == 0:
                        if some(n := g * GB + b):
                            eng.wait_ge(att_ok, n)
                    for j in range(HPC):
                        hh = c * HPC + j
                        last = eng.matmul(bank_o[:, hh * VW:(hh + 1) * VW], prT[:, q % 2, j, :], v[:, b, hh, :],
                                          start=True, stop=True)
                    last.then_inc(o_mm, 1)
                elif u[0] == "D":
                    c = u[1]
                    if c == 0:
                        eng.wait_ge(pt_sb, (g + 1) * NQ)
                    elif c == 1:
                        eng.wait_ge(att_ok, (g + 1) * GB)
                    else:
                        eng.wait_ge(s_sb, (g + 1) * NQ)
                    for b in range(GB):
                        eng.wait_ge(x1_ok, g * GB + b + 1)
                        last = eng.transpose(d_banks[c][:, b * N:(b + 1) * N], xn[:, b, c * P:(c + 1) * P], ident[:, :])
                    last.then_inc(x1T_mm, 1)
                elif u[0] == "N":
                    l, k = u[1], u[2]
                    side, m = divmod(k, DC)
                    if l == 0:
                        if k == 0:
                            eng.wait_ge(x1T_lo_ok, (h + 1) * DC)
                            if some(n := h * (GB * L)):
                                eng.wait_ge(c_sb, n)
                    elif k == 0:
                        eng.wait_ge(h1_lo_ok, (h + 1) * DC)
                    if k >= 2:
                        eng.wait_ge(n_sb, h * (2 * DC * L) + 2 * DC * l + k - 1)
                    if isinstance(h, int) and h == 0:
                        eng.wait_ge(w1_lo_done, 3 * L)
                    cols = slice(m * P, (m + 1) * P)
                    split_product(nh_bank(l, k)[:, :],
                                  lambda c: w1_hi[:, l, side, c, cols], lambda c: w1_lo[:, l, side, c, cols],
                                  lambda c: hT_hi[:, c, :], lambda c: hT_lo[:, c, :]).then_inc(n_mm, 1)
                elif u[0] == "H":
                    l, b = u[1], u[2]
                    if b < 2:
                        eng.wait_ge(n_sb, h * (2 * DC * L) + 2 * DC * (l + 1) - 1 + b)
                    else:
                        eng.wait_ge(hl_sb, h * (GB * L) + GB * l + b - 1)
                    rows = slice(b * N, (b + 1) * N)
                    split_product(nh_bank(l, b)[:, 0:D],
                                  lambda c: hT_hi[:, c, rows], lambda c: hT_lo[:, c, rows],
                                  lambda c: w1_hi[:, l, 2, c, :], lambda c: w1_lo[:, l, 2, c, :]).then_inc(hl_mm, 1)
                elif u[0] == "U":
                    l, p = u[1], u[2]
                    eng.wait_ge(n_sb, h * (2 * DC * L) + 2 * DC * (l + 1))
                    if l == 0:
                        eng.wait_ge(hT0_ok, h + 1)
                    else:
                        eng.wait_ge(h1_ok, (h + 1) * DC)
                    if some(n := h * (2 * L) + 2 * l + p):
                        eng.wait_ge(u_sb, n)
                    for b in (2 * p, 2 * p + 1):
                        for c in range(DC):
                            last = eng.matmul(bank_u[:, (b % 2) * 2 * N:(b % 2 + 1) * 2 * N],
                                              hT[:, c, b * N:(b + 1) * N], nT[:, c, :, b * N:(b + 1) * N],
                                              start=(c == 0), stop=(c == DC - 1))
                    last.then_inc(u_mm, 1)
                elif u[0] == "C":
                    l, b = u[1], u[2]
                    eng.wait_ge(e_ok, h * (2 * L) + 2 * l + b // 2 + 1)
                    eng.wait_ge(hl_sb, h * (GB * L) + GB * (l + 1))
                    if b >= 2:
                        eng.wait_ge(c_sb, h * (GB * L) + GB * l + b - 1)
                    elif l == 1:
                        eng.wait_ge(h1_ok, (h + 1) * DC)
                    eng.matmul(c_banks[b % 2][:, 0:D + 1], uc[:, b, :], hl[:, b, :], start=True, stop=True).then_inc(c_mm, 1)
                elif u[0] == "W":
                    c = u[1]
                    if c == 0:
                        eng.wait_ge(u_sb, h * (2 * L) + 2)
                    elif c == 1:
                        eng.wait_ge(c_sb, h * (GB * L) + GB)
                    for b in range(GB):
                        eng.wait_ge(y_ok, h * GB + b + 1)
                        last = eng.transpose(w_banks[c][:, b * N:(b + 1) * N], cs[:, b, c * P:(c + 1) * P], ident[:, :])
                    last.then_inc(yT_mm, 1)

            eng.wait_ge(ld_w0, 7 * 16)
            eng.wait_ge(const_done, 5)
            over_turns(eng, unit)


_OUT = ("out_dram", (G, P, GB, D))


def kernel(**inputs):
    import concourse.bacc as _bacc
    from concourse import mybir as _mybir
    from concourse.bass_utils import run_bass_kernel_spmd as _run

    a = {k: np.ascontiguousarray(x) for k, x in inputs.items()}
    x, adj = a["x"], a["adj"]
    grouped = x.reshape(G, GB, N, D)
    pairs = adj.reshape(G, GB, N, N)

    def columns(b):
        return b.reshape(DC, P).T

    arrays = {
        "xT_in": grouped.reshape(G, T, DC, P).transpose(0, 3, 2, 1),
        "xn_in": grouped.transpose(0, 2, 1, 3),
        "adj_in": pairs.transpose(0, 2, 1, 3),
        "adjT_in": pairs.transpose(0, 3, 1, 2),
        "wq_in": a["L0_gnn_Wq"], "wk_in": a["L0_gnn_Wk"], "wv_in": a["L0_gnn_Wv"],
        "bq_in": columns(a["L0_gnn_bq"]), "bk_in": columns(a["L0_gnn_bk"]), "bv_in": a["L0_gnn_bv"],
        "beta_in": a["L0_gnn_beta"].reshape(1),
        "wl_in": a["L1_gnn_W_left"], "wr_in": a["L1_gnn_W_right"],
        "wlin_in": a["L1_gnn_W_lin"].transpose(0, 2, 1),
        "blin_in": a["L1_gnn_b_lin"],
        "lna_col_in": columns(a["L1_gnn_ln_a"][0]), "lnb_col_in": columns(a["L1_gnn_ln_b"][0]),
        "lna_in": a["L1_gnn_ln_a"][1], "lnb_in": a["L1_gnn_ln_b"][1],
    }
    arrays = {k: np.ascontiguousarray(w) for k, w in arrays.items()}
    nc = _bacc.Bacc("TRN2", target_bir_lowering=False, num_devices=1)
    args = [nc.dram_tensor(k, w.shape, _mybir.dt.from_np(w.dtype), kind="ExternalInput").ap() for k, w in arrays.items()]
    args.append(nc.dram_tensor(_OUT[0], _OUT[1], F32, kind="ExternalOutput").ap())
    graph_blocks(nc, *args)
    r = _run(nc, [arrays], core_ids=[0])
    got = r.results[0][_OUT[0]]
    return np.ascontiguousarray(got.transpose(0, 2, 1, 3)).reshape(NB, N, D)
```

```python
from contextlib import ExitStack

import numpy as np

import concourse.bass as bass
from concourse import mybir

F32 = mybir.dt.float32
F32R = mybir.dt.float32r
ALU = mybir.AluOpType
ACT = mybir.ActivationFunctionType
AX = mybir.AxisListType

P = 128
NB, N, D = 64, 128, 384
H = 12
HD = D // H
GB = 4
G = NB // GB
T = GB * N
DC = D // P
HPC = P // HD
NQ = GB * DC
L = 2
VW = HD + 1
MASKED = -9000000000000000.0
LN_EPS, L1_EPS, SUM_EPS = 1e-5, 1e-3, 1e-10


def turn():
    return [
        (0, ("K", 2)),
        (0, ("S", 0)),
        (0, ("S", 1)), (0, ("K", 3)), (0, ("Q", 0)), (-1, ("N", 1, 0)),
        (0, ("S", 2)), (0, ("Q", 1)), (0, ("K", 4)), (-1, ("N", 1, 1)), (0, ("Q", 2)),
        (0, ("S", 3)), (0, ("T", 0)), (-1, ("N", 1, 2)), (0, ("K", 5)), (0, ("Q", 3)),
        (0, ("S", 4)), (0, ("T", 1)), (0, ("V", 0)), (-1, ("N", 1, 3)), (0, ("K", 6)), (-1, ("U", 1, 0)),
        (0, ("Q", 4)),
        (0, ("S", 5)), (0, ("V", 1)), (0, ("T", 2)), (0, ("K", 7)), (-1, ("N", 1, 4)), (0, ("Q", 5)),
        (0, ("S", 6)), (0, ("T", 3)), (0, ("V", 2)), (-1, ("U", 1, 1)), (0, ("Q", 6)), (0, ("K", 8)),
        (0, ("S", 7)), (0, ("T", 4)), (0, ("V", 3)), (-1, ("N", 1, 5)), (0, ("Q", 7)),
        (0, ("S", 8)), (0, ("K", 9)), (0, ("T", 5)), (0, ("V", 4)), (0, ("K", 10)), (-1, ("H", 1, 0)), (0, ("Q", 8)),
        (0, ("V", 5)), (0, ("T", 6)),
        (0, ("S", 9)), (0, ("K", 11)), (-1, ("U", 1, 2)), (-1, ("M", 1, 0)), (-1, ("M", 1, 1)), (0, ("Q", 9)),
        (0, ("T", 7)),
        (0, ("S", 10)), (0, ("V", 6)), (-1, ("E", 1, 0)),
        (0, ("S", 11)), (-1, ("H", 1, 1)), (1, ("P", 0)), (0, ("T", 8)), (0, ("V", 7)), (-1, ("E", 1, 1)),
        (0, ("Q", 10)), (-1, ("H", 1, 2)), (1, ("P", 1)), (0, ("V", 8)), (0, ("Q", 11)), (0, ("T", 9)),
        (-1, ("H", 1, 3)), (1, ("P", 2)), (0, ("T", 10)), (0, ("V", 9)), (-1, ("C", 1, 0)), (0, ("T", 11)),
        (0, ("V", 10)), (-1, ("C", 1, 1)), (0, ("V", 11)),
        (0, ("X", 0)), (-1, ("C", 1, 2)), (1, ("A", 0)), (-1, ("C", 1, 3)), (0, ("X", 1)), (1, ("A", 1)),
        (0, ("D", 0)), (0, ("D", 1)), (0, ("D", 2)), (-1, ("F", 0)), (-1, ("F", 1)), (1, ("A", 2)), (-1, ("F", 2)),
        (0, ("N", 0, 0)), (-1, ("F", 3)), (0, ("N", 0, 1)), (-1, ("F", 4)), (0, ("N", 0, 2)), (0, ("U", 0, 0)),
        (0, ("R", 0)), (-1, ("F", 5)), (-1, ("F", 6)), (0, ("N", 0, 3)), (-1, ("F", 7)), (0, ("N", 0, 4)),
        (-1, ("F", 8)), (0, ("N", 0, 5)), (-1, ("F", 9)), (-1, ("F", 10)), (0, ("H", 0, 0)), (-1, ("F", 11)),
        (0, ("U", 0, 1)), (0, ("U", 0, 2)), (0, ("H", 0, 1)), (0, ("M", 0, 0)), (0, ("M", 0, 1)), (0, ("E", 0, 0)),
        (0, ("H", 0, 2)), (0, ("H", 0, 3)), (1, ("A", 3)), (0, ("C", 0, 0)), (0, ("E", 0, 1)), (0, ("C", 0, 1)),
        (1, ("A", 4)), (0, ("C", 0, 2)), (0, ("C", 0, 3)), (1, ("A", 5)), (0, ("Y", 0)), (1, ("B", 0)), (0, ("Y", 1)),
        (1, ("B", 1)), (0, ("Y", 2)), (0, ("Y", 3)), (0, ("Y", 4)), (0, ("Y", 5)), (1, ("B", 2)), (1, ("K", 0)),
        (0, ("W", 0)), (0, ("W", 1)), (0, ("W", 2)), (1, ("B", 3)), (1, ("K", 1)),
    ]


def graph_blocks(nc, xT_d, xn_d, adj_d, adjT_d, wq_d, wk_d, wv_d, bq_d, bk_d, bv_d, beta_d,
                 wl_d, wr_d, wlin_d, blin_d, lna_col_d, lnb_col_d, lna_d, lnb_d, out_d):
    with ExitStack() as ctx:
        def sb(name, shape, dt=F32):
            return ctx.enter_context(nc.sbuf_tensor(name, shape, dt))

        def bank(name):
            return ctx.enter_context(nc.psum_tensor(name, [P, 512], F32))

        def sem(name):
            return ctx.enter_context(nc.semaphore(name))

        w0_hi = sb("w0_hi", [P, 3, DC, D], F32R)
        w0_lo = sb("w0_lo", [P, 3, DC, D], F32R)
        w1_hi = sb("w1_hi", [P, L, 3, DC, D], F32R)
        w1_lo = sb("w1_lo", [P, L, 3, DC, D], F32R)
        bqk = sb("bqk", [P, 2, DC])
        bv_b = sb("bv_b", [P, D])
        blin_b = sb("blin_b", [P, L, D])
        lna_b = sb("lna_b", [P, D])
        lnb_b = sb("lnb_b", [P, D])
        lna_c = sb("lna_c", [P, DC])
        lnb_c = sb("lnb_c", [P, DC])
        beta = sb("beta", [P, 1])
        ident = sb("ident", [P, P])
        half = sb("half", [P, 2, GB])

        xT_hi = sb("xT_hi", [P, DC, T], F32R)
        xT_lo = sb("xT_lo", [P, DC, T], F32R)
        xn = sb("xn", [P, GB, D])
        adj = sb("adj", [P, GB, N])
        bias = sb("bias", [P, GB, N])
        qT_hi = sb("qT_hi", [P, DC, T], F32R)
        qT_lo = sb("qT_lo", [P, DC, T], F32R)
        kT = sb("kT", [P, DC, T])
        v = sb("v", [P, GB, H, VW])
        kz_hi = sb("kz_hi", [P, 2, HPC, N], F32R)
        kz_lo = sb("kz_lo", [P, 2, HPC, N], F32R)
        pr = sb("pr", [P, 3, HPC, N])
        nmax = sb("nmax", [P, 3, HPC])
        prT = sb("prT", [P, 2, HPC, N])
        rden = sb("rden", [P, 2, H])
        att = sb("att", [P, D])
        st0 = sb("st0", [P, GB, 6])
        mv0 = sb("mv0", [P, GB, 2])
        ve0 = sb("ve0", [P, GB])
        rs0 = sb("rs0", [P, GB])

        hT_hi = sb("hT_hi", [P, DC, T], F32R)
        hT_lo = sb("hT_lo", [P, DC, T], F32R)
        adjT = sb("adjT", [P, GB, N])
        tri = sb("tri", [P, GB, 2, N])
        nT_hi = sb("nT_hi", [P, 2, 2, T], F32R)
        nT_lo = sb("nT_lo", [P, 2, 2, T], F32R)
        hl = sb("hl", [P, GB, D + 1])
        uw = sb("uw", [P, 2, 2, N])
        uc = sb("uc", [P, GB, N])
        cs = sb("cs", [P, GB, D + 1])
        st1 = sb("st1", [P, GB, 6])
        mv1 = sb("mv1", [P, GB, 2])
        sc = sb("sc", [P, 5, GB])
        stf = sb("stf", [P, GB, 6])
        mvf = sb("mvf", [P, GB, 2])
        rsf = sb("rsf", [P, 2, GB])

        bank_p0, bank_s0, bank_s1, bank_t, bank_o, bank_p1, bank_u, bank_c = (
            bank(n) for n in ("bank_p0", "bank_s0", "bank_s1", "bank_t", "bank_o", "bank_p1", "bank_u", "bank_c"))
        bank_s = [bank_s0, bank_s1]
        d_banks = [bank_t, bank_o, bank_s0]
        w_banks = [bank_u, bank_c, bank_p1]
        c_banks = [bank_c, bank_p1]
        u_banks = [bank_c, bank_u]
        proj_banks = [bank_s1, bank_p0]

        def nh_bank(l, k):
            return (bank_p1, bank_p0 if l else bank_o)[k % 2]

        ld_w0 = sem("ld_w0")
        ld_w1 = sem("ld_w1")
        ld_w0s = [sem(f"ld_w0s{i}") for i in range(3)]
        ld_w1s = [sem(f"ld_w1s{i}") for i in range(3 * L)]
        w0_hi_done = sem("w0_hi_done")
        w0_lo_done = sem("w0_lo_done")
        w1_hi_done = sem("w1_hi_done")
        w1_lo_done = sem("w1_lo_done")
        const_done = sem("const_done")
        ident_zero = sem("ident_zero")
        ld_xT = sem("ld_xT")
        ld_xn = sem("ld_xn")
        ld_adj = sem("ld_adj")
        ld_adjT = sem("ld_adjT")
        xT_hi_ok = sem("xT_hi_ok")
        xT_lo_ok = sem("xT_lo_ok")
        st_out = sem("st_out")
        qk_mm = sem("qk_mm")
        qk_sb = sem("qk_sb")
        q_lo_ok = sem("q_lo_ok")
        zeros = sem("zeros")
        kz_zero = sem("kz_zero")
        kz_hi_ok = sem("kz_hi_ok")
        kz_lo_ok = sem("kz_lo_ok")
        v_mm = sem("v_mm")
        v_sb = sem("v_sb")
        pen_ok = sem("pen_ok")
        bias_ok = sem("bias_ok")
        s_mm = sem("s_mm")
        s_sb = sem("s_sb")
        nmax_ok = sem("nmax_ok")
        exp_ok = sem("exp_ok")
        pt_mm = sem("pt_mm")
        pt_sb = sem("pt_sb")
        o_mm = sem("o_mm")
        rden_ok = sem("rden_ok")
        att_ok = sem("att_ok")
        res0_ok = sem("res0_ok")
        st0_ok = sem("st0_ok")
        mv0_ok = sem("mv0_ok")
        ve0_ok = sem("ve0_ok")
        rs0_ok = sem("rs0_ok")
        x1_ok = sem("x1_ok")
        x1T_mm = sem("x1T_mm")
        x1T_hi_ok = sem("x1T_hi_ok")
        x1T_lo_ok = sem("x1T_lo_ok")
        x1_kept = sem("x1_kept")
        ld_x1 = sem("ld_x1")
        tri_ok = sem("tri_ok")
        n_mm = sem("n_mm")
        n_hi_ok = sem("n_hi_ok")
        n_lo_ok = sem("n_lo_ok")
        hl_mm = sem("hl_mm")
        hl_sb = sem("hl_sb")
        u_mm = sem("u_mm")
        u_sb = sem("u_sb")
        ut_ok = sem("ut_ok")
        ue_ok = sem("ue_ok")
        e_ok = sem("e_ok")
        c_mm = sem("c_mm")
        c_sb = sem("c_sb")
        st1_ok = sem("st1_ok")
        mv1_ok = sem("mv1_ok")
        sc_ok = sem("sc_ok")
        sd_ok = sem("sd_ok")
        y_ok = sem("y_ok")
        yT_mm = sem("yT_mm")
        h1_ok = sem("h1_ok")
        h1_hi_ok = sem("h1_hi_ok")
        h1_lo_ok = sem("h1_lo_ok")
        fa_ok = sem("fa_ok")
        fb_ok = sem("fb_ok")
        res1_ok = sem("res1_ok")
        stf_ok = sem("stf_ok")
        mvf_ok = sem("mvf_ok")
        vef_ok = sem("vef_ok")
        rsf_ok = sem("rsf_ok")
        carrier = sem("carrier")
        out_ok = sem("out_ok")

        def some(value):
            return not isinstance(value, int) or value > 0

        def alone(eng):
            eng.sem_inc(carrier, 1)

        block = ctx.enter_context(nc.Block())

        x_in = cs[:, :, :].rearrange("p b d -> p (b d)")
        pr_flat = pr[:, :, :, :].rearrange("p s j n -> p (s j n)")
        x1 = pr_flat.rearrange("p (b d) -> p b d", b=GB)
        x_pr = pr_flat.rearrange("p (c t) -> p c t", c=DC)

        w0_src = [w.rearrange("(c p) n -> p c n", p=P) for w in (wq_d, wk_d, wv_d)]
        w0_stage = [hl[:, 0:DC, 0:D], kT[:, :, 0:D], pr_flat[:, 0:DC * D].rearrange("p (c n) -> p c n", c=DC)]
        w1_stage = [hl[:, 0:DC, 0:D], cs[:, 0:DC, 0:D]]
        w1_src = [w[l].rearrange("(c p) n -> p c n", p=P) for l in range(L) for w in (wl_d, wr_d, wlin_d)]

        def over_turns(eng, unit):
            for i in (-1, 0):
                for shift, u in turn():
                    if i + shift >= 0:
                        unit(u, i + shift)
                    if i == 0 and u[0] == "S" and 0 <= u[1] - 2 < 3 * L:
                        unit(("G", u[1] - 2), 0)
            with eng.Fori(1, G - 1) as i:
                for shift, u in turn():
                    unit(u, i + shift)
            for i in (G - 1, G):
                for shift, u in turn():
                    if i + shift < G:
                        unit(u, i + shift)

        @block.sync
        def _(eng):
            def load_xT(g):
                if isinstance(g, int) and g == 1:
                    eng.wait_ge(w1_lo_done, 3 * L)
                elif some(n := (g - 1) * DC):
                    eng.wait_ge(yT_mm, n)
                    alone(eng)
                eng.dma_start(x_in[:, 0:DC * T], xT_d[g]).then_inc(ld_xT, 16)

            def load_adj(g):
                if some(n := g * 2):
                    eng.wait_ge(tri_ok, n)
                    alone(eng)
                eng.dma_start(adj[:, :, :], adj_d[g]).then_inc(ld_adj, 16)

            def load_xn(g):
                if some(n := g):
                    eng.wait_ge(x1_kept, n * 16)
                    alone(eng)
                    eng.wait_ge(x1T_mm, g * DC)
                    alone(eng)
                eng.dma_start(xn[:, :, :], xn_d[g]).then_inc(ld_xn, 16)

            def load_adjT(h):
                if some(n := h * (2 * L)):
                    eng.wait_ge(e_ok, n)
                    alone(eng)
                eng.dma_start(adjT[:, :, :], adjT_d[h]).then_inc(ld_adjT, 16)

            def keep_x1(h):
                eng.wait_ge(x1_ok, (h + 1) * GB)
                alone(eng)
                eng.dma_start(out_d[h], xn[:, :, :]).then_inc(x1_kept, 16)

            def load_x1(h):
                eng.wait_ge(x1_kept, (h + 1) * 16)
                alone(eng)
                if isinstance(h, int) and h == G - 1:
                    eng.wait_ge(h1_lo_ok, (h + 1) * DC)
                else:
                    eng.wait_ge(pt_mm, (h + 2) * NQ)
                    alone(eng)
                eng.dma_start(x1, out_d[h]).then_inc(ld_x1, 16)

            def store(h):
                eng.wait_ge(out_ok, (h + 1) * GB)
                alone(eng)
                eng.dma_start(out_d[h], cs[:, :, 0:D]).then_inc(st_out, 16)

            load_xT(0)
            for i in range(3):
                eng.dma_start(w0_stage[i], w0_src[i]).then_inc(ld_w0s[i], 16)
                if i == 0:
                    eng.dma_start(bqk[:, 0, :], bq_d).then_inc(ld_w0, 16)
                    eng.dma_start(bqk[:, 1, :], bk_d).then_inc(ld_w0, 16)
            load_adj(0)
            eng.dma_start(bv_b[:, :], bv_d.partition_broadcast(P)).then_inc(ld_w0, 16)
            eng.dma_start(beta[:, :], beta_d.partition_broadcast(P)).then_inc(ld_w0, 16)
            load_xn(0)
            for l in range(L):
                eng.dma_start(blin_b[:, l, :], blin_d[l].partition_broadcast(P)).then_inc(ld_w1, 16)
            eng.dma_start(lna_b[:, :], lna_d.partition_broadcast(P)).then_inc(ld_w1, 16)
            eng.dma_start(lnb_b[:, :], lnb_d.partition_broadcast(P)).then_inc(ld_w1, 16)
            eng.dma_start(lna_c[:, :], lna_col_d).then_inc(ld_w1, 16)
            eng.dma_start(lnb_c[:, :], lnb_col_d).then_inc(ld_w1, 16)
            load_adjT(0)
            for i in range(3 * L):
                if i == 0:
                    eng.wait_ge(w0_lo_done, 1)
                elif i == 1:
                    eng.wait_ge(xT_lo_ok, DC)
                else:
                    eng.wait_ge(w1_lo_done, i - 1)
                eng.dma_start(w1_stage[i % 2], w1_src[i]).then_inc(ld_w1s[i], 16)
            load_xT(1)
            keep_x1(0)
            load_adj(1)
            with eng.Fori(1, G - 1) as i:
                load_xn(i)
                load_xT(i + 1)
                load_adjT(i)
                load_x1(i - 1)
                keep_x1(i)
                load_adj(i + 1)
                store(i - 1)
            load_xn(G - 1)
            load_adjT(G - 1)
            load_x1(G - 2)
            keep_x1(G - 1)
            store(G - 2)
            load_x1(G - 1)
            store(G - 1)
            eng.wait_ge(st_out, 16 * G)

        @block.gpsimd
        def _(eng):
            eng.memset(ident[:, :], 0.0).then_inc(ident_zero, 1)
            eng.memset(half[:, 0, :], -0.5).then_inc(const_done, 1)
            eng.memset(half[:, 1, :], 0.5).then_inc(const_done, 1)
            eng.memset(v[:, :, :, HD:VW], 1.0).then_inc(const_done, 1)
            eng.memset(hl[:, :, D:D + 1], 1.0).then_inc(const_done, 1)
            eng.wait_ge(ident_zero, 1)
            eng.affine_select(out=ident[:, :], in_=ident[:, :], compare_op=ALU.not_equal, fill=1.0,
                              base=0, pattern=[[-1, P]], channel_multiplier=1).then_inc(const_done, 1)
            eng.memset(bias[:, :, :], 0.0).then_inc(zeros, 1)

            def unit(u, g):
                h = g
                if u[0] == "G":
                    i = u[1]
                    eng.wait_ge(w1_hi_done, i + 1)
                    eng.tensor_tensor(w1_lo[:, i // 3, i % 3, :, :], w1_stage[i % 2],
                                      w1_hi[:, i // 3, i % 3, :, :].bitcast(F32), ALU.subtract).then_inc(w1_lo_done, 1)
                elif u[0] == "P":
                    c = u[1]
                    eng.wait_ge(xT_hi_ok, g * DC + c + 1)
                    eng.tensor_tensor(xT_lo[:, c, :], x_in[:, c * T:(c + 1) * T], xT_hi[:, c, :].bitcast(F32),
                                      ALU.subtract).then_inc(xT_lo_ok, 1)
                elif u[0] == "V" and u[1] % DC == DC - 1:
                    b = u[1] // DC
                    eng.wait_ge(att_ok, g * GB + b + 1)
                    eng.wait_ge(ld_xn, (g + 1) * 16)
                    eng.tensor_tensor(xn[:, b, :], xn[:, b, :], att[:, :], ALU.add).then_inc(res0_ok, 1)
                elif u[0] == "X" and u[1] == 0:
                    eng.wait_ge(ve0_ok, g + 1)
                    if some(n := g * GB):
                        eng.wait_ge(x1_ok, n)
                    eng.tensor_tensor(rs0[:, :], ve0[:, :], half[:, 0, :], ALU.pow).then_inc(rs0_ok, 1)
                elif u == ("R", 0):
                    eng.wait_ge(ld_adj, (h + 1) * 16)
                    eng.wait_ge(ld_adjT, (h + 1) * 16)
                    if some(n := h * (2 * L)):
                        eng.wait_ge(u_sb, n)
                    alone(eng)
                    eng.affine_select(out=tri[:, :, 0, :], in_=adjT[:, :, :], compare_op=ALU.is_ge, fill=0.0,
                                      base=0, pattern=[[0, GB], [-1, N]], channel_multiplier=1).then_inc(tri_ok, 1)
                    eng.affine_select(out=tri[:, :, 1, :], in_=adj[:, :, :], compare_op=ALU.is_gt, fill=0.0,
                                      base=0, pattern=[[0, GB], [1, N]], channel_multiplier=-1).then_inc(tri_ok, 1)
                elif u[0] == "W":
                    c = u[1]
                    eng.wait_ge(h1_hi_ok, h * DC + c + 1)
                    eng.tensor_tensor(hT_lo[:, c, :], x_pr[:, c, :], hT_hi[:, c, :].bitcast(F32),
                                      ALU.subtract).then_inc(h1_lo_ok, 1)
                elif u == ("Y", 0):
                    sd(0, h)
                elif u == ("F", 0):
                    sd(L - 1, h)
                elif u == ("F", 2 * GB + 2):
                    eng.wait_ge(vef_ok, h + 1)
                    eng.tensor_tensor(rsf[:, 1, :], rsf[:, 0, :], half[:, 0, :], ALU.pow).then_inc(rsf_ok, 1)

            def sd(l, h):
                eng.wait_ge(sc_ok, h * (4 * L) + 4 * l + 1)
                eng.tensor_tensor(sc[:, 1, :], sc[:, 0, :], half[:, 1, :], ALU.pow).then_inc(sd_ok, 1)

            eng.wait_ge(const_done, 5)
            over_turns(eng, unit)

        @block.scalar
        def _(eng):
            def unit(u, g):
                h = g
                if u[0] == "P":
                    c = u[1]
                    eng.wait_ge(ld_xT, (g + 1) * 16)
                    if some(n := g * GB):
                        eng.wait_ge(v_mm, n)
                    eng.activation(xT_hi[:, c, :], x_in[:, c * T:(c + 1) * T], ACT.Copy).then_inc(xT_hi_ok, 1)
                elif u[0] == "A":
                    i, c = divmod(u[1], DC)
                    if isinstance(g, int) and g == 0:
                        eng.wait_ge(ld_w0, 4 * 16)
                    eng.wait_ge(qk_mm, g * (2 * DC) + u[1] + 1)
                    if some(n := g * NQ):
                        eng.wait_ge(s_mm, n)
                    eng.activation(kT[:, c, :] if i else qT_hi[:, c, :], proj_banks[u[1] % 2][:, :], ACT.Identity,
                                   bias=bqk[:, i, c:c + 1]).then_inc(qk_sb, 1)
                elif u[0] == "K":
                    q = u[1]
                    b, c = divmod(q, DC)
                    if q == 0:
                        if isinstance(g, int) and g == 0:
                            eng.wait_ge(kz_zero, 4)
                        eng.wait_ge(qk_sb, (g + 1) * (2 * DC))
                    if some(n := g * NQ + q - 1):
                        eng.wait_ge(s_mm, n)
                    for j in range(HPC):
                        rows = slice(j * HD, (j + 1) * HD)
                        eng.activation(kz_hi[rows, q % 2, j, :], kT[rows, c, b * N:(b + 1) * N],
                                       ACT.Copy).then_inc(kz_hi_ok, 1)
                elif u[0] == "Q":
                    q = u[1]
                    eng.wait_ge(nmax_ok, g * NQ + q + 1)
                    for j in range(HPC):
                        last = eng.activation(pr[:, q % 3, j, :], pr[:, q % 3, j, :], ACT.Exp,
                                              bias=nmax[:, q % 3, j:j + 1])
                    last.then_inc(exp_ok, 1)
                elif u[0] == "T":
                    q = u[1]
                    eng.wait_ge(pt_mm, g * NQ + q + 1)
                    if some(n := g * NQ + q - 1):
                        eng.wait_ge(o_mm, n)
                    eng.activation(prT[:, q % 2, :, :], bank_t[:, :], ACT.Copy).then_inc(pt_sb, 1)
                elif u[0] == "D":
                    c = u[1]
                    eng.wait_ge(x1T_mm, g * DC + c + 1)
                    if some(n := g * (L * GB)):
                        eng.wait_ge(hl_mm, n)
                        eng.wait_ge(u_mm, g * (L * DC))
                    eng.activation(hT_hi[:, c, :], d_banks[c][:, :], ACT.Copy).then_inc(x1T_hi_ok, 1)
                elif u[0] == "N":
                    l, k = u[1], u[2]
                    m, side = divmod(k, 2)
                    eng.wait_ge(n_mm, h * (2 * DC * L) + 2 * DC * l + k + 1)
                    if some(n := h * (L * DC) + DC * l + (m - 1 if m else 0)):
                        eng.wait_ge(u_mm, n)
                    eng.activation(nT_hi[:, m % 2, side, :], nh_bank(l, k)[:, :], ACT.Copy).then_inc(n_hi_ok, 1)
                elif u[0] == "E":
                    l, p = u[1], u[2]
                    eng.wait_ge(ut_ok, h * (2 * L) + 2 * l + p + 1)
                    eng.activation(uc[:, 2 * p:2 * p + 2, :], uc[:, 2 * p:2 * p + 2, :], ACT.Exp,
                                   scale=float(1.0 / np.sqrt(D))).then_inc(ue_ok, 1)
                elif u[0] == "C":
                    l, b = u[1], u[2]
                    eng.wait_ge(c_mm, h * (GB * L) + GB * l + b + 1)
                    if l == 0:
                        if some(n := h * 16):
                            eng.wait_ge(st_out, n)
                    else:
                        eng.wait_ge(xT_lo_ok, (min(h + 3, G) if isinstance(h, int) else h + 3) * DC)
                        eng.wait_ge(yT_mm, (h + 1) * DC)
                    eng.activation(cs[:, b, :], c_banks[b % 2][:, 0:D + 1], ACT.Copy).then_inc(c_sb, 1)
                elif u[0] == "W":
                    c = u[1]
                    eng.wait_ge(yT_mm, h * DC + c + 1)
                    eng.wait_ge(pt_mm, (h + 1) * NQ)
                    if some(n := h * GB):
                        eng.wait_ge(res1_ok, n)
                    eng.activation(x_pr[:, c, :], w_banks[c][:, :], ACT.Relu, bias=lnb_c[:, c:c + 1],
                                   scale=lna_c[:, c:c + 1]).then_inc(h1_ok, 1)

            over_turns(eng, unit)

        @block.vector
        def _(eng):
            def make_bias(g):
                eng.wait_ge(ld_adj, (g + 1) * 16)
                if some(n := g * NQ):
                    eng.wait_ge(s_sb, n)
                eng.tensor_scalar(bias[:, :, :], adj[:, :, :], 0.0, MASKED, ALU.is_le, ALU.mult).then_inc(pen_ok, 1)
                eng.wait_ge(pen_ok, g + 1)
                eng.scalar_tensor_tensor(out=bias[:, :, :], in0=adj[:, :, :], scalar=beta[:, 0:1], in1=bias[:, :, :],
                                         op0=ALU.mult, op1=ALU.add).then_inc(bias_ok, 1)

            def unit(u, g):
                h = g
                if u[0] == "G":
                    i = u[1]
                    eng.wait_ge(ld_w1s[i], 16)
                    eng.tensor_copy(w1_hi[:, i // 3, i % 3, :, :], w1_stage[i % 2]).then_inc(w1_hi_done, 1)
                elif u == ("A", 5):
                    make_bias(g)
                elif u[0] == "A" and u[1] < DC:
                    c = u[1]
                    eng.wait_ge(qk_sb, g * (2 * DC) + c + 1)
                    eng.scalar_tensor_tensor(out=qT_lo[:, c, :], in0=proj_banks[c % 2][:, :], scalar=bqk[:, 0, c:c + 1],
                                             in1=qT_hi[:, c, :].bitcast(F32), op0=ALU.add,
                                             op1=ALU.subtract).then_inc(q_lo_ok, 1)
                elif u[0] == "K":
                    q = u[1]
                    b, c = divmod(q, DC)
                    for j in range(HPC):
                        rows = slice(j * HD, (j + 1) * HD)
                        eng.wait_ge(kz_hi_ok, g * (NQ * HPC) + q * HPC + j + 1)
                        eng.tensor_tensor(kz_lo[rows, q % 2, j, :], kT[rows, c, b * N:(b + 1) * N],
                                          kz_hi[rows, q % 2, j, :].bitcast(F32), ALU.subtract).then_inc(kz_lo_ok, 1)
                elif u[0] == "B":
                    b = u[1]
                    eng.wait_ge(v_mm, g * GB + b + 1)
                    if some(n := g * NQ + DC * (b + 1) - NQ):
                        eng.wait_ge(o_mm, n)
                    eng.tensor_tensor(v[:, b, :, 0:HD],
                                      proj_banks[b % 2][:, 0:D].rearrange("p (h d) -> p h d", h=H),
                                      bv_b[:, :].rearrange("p (h d) -> p h d", h=H), ALU.add).then_inc(v_sb, 1)
                elif u[0] == "S":
                    q = u[1]
                    b = q // DC
                    eng.wait_ge(s_mm, g * NQ + q + 1)
                    if some(n := g * NQ + q - 2):
                        eng.wait_ge(pt_mm, n)
                    if q < 3:
                        if some(n := g * DC):
                            eng.wait_ge(h1_lo_ok, n)
                    eng.wait_ge(bias_ok, g + 1)
                    eng.scalar_tensor_tensor(
                        out=pr[:, q % 3, :, :], in0=bank_s[q % 2][:, :].rearrange("p (t n) -> p t n", t=HPC),
                        scalar=float(1.0 / np.sqrt(HD)),
                        in1=bias[:, b:b + 1, :].to_broadcast([P, HPC, N]), op0=ALU.mult, op1=ALU.add).then_inc(s_sb, 1)
                    eng.wait_ge(s_sb, g * NQ + q + 1)
                    eng.tensor_reduce(nmax[:, q % 3, :], pr[:, q % 3, :, :], AX.X, ALU.max,
                                      negate=True).then_inc(nmax_ok, 1)
                elif u[0] == "V":
                    q = u[1]
                    b = q // DC
                    if q % DC == DC - 1:
                        o = bank_o[:, 0:H * VW].rearrange("p (h d) -> p h d", h=H)
                        eng.wait_ge(o_mm, g * NQ + q + 1)
                        eng.reciprocal(rden[:, b % 2, :], o[:, :, HD]).then_inc(rden_ok, 1)
                        eng.wait_ge(rden_ok, g * GB + b + 1)
                        if some(n := g * GB + b):
                            eng.wait_ge(res0_ok, n)
                        eng.tensor_tensor(att[:, :].rearrange("p (h d) -> p h d", h=H), o[:, :, 0:HD],
                                          rden[:, b % 2, :].unsqueeze(2).to_broadcast([P, H, HD]),
                                          ALU.mult).then_inc(att_ok, 1)
                    if b > 0 and q % DC == 1:
                        stats0(g, b - 1)
                elif u == ("X", 0):
                    if isinstance(g, int) and g == 0:
                        eng.wait_ge(ld_w1, 6 * 16)
                    stats0(g, GB - 1)
                    for b in range(GB):
                        eng.wait_ge(st0_ok, g * GB + b + 1)
                        alone(eng)
                        last = eng.bn_aggr(mv0[:, b, :], st0[:, b, :])
                    last.then_inc(mv0_ok, 1)
                    eng.wait_ge(mv0_ok, g + 1)
                    eng.tensor_scalar(ve0[:, :], mv0[:, :, 1], LN_EPS, None, ALU.add).then_inc(ve0_ok, 1)
                elif u == ("X", 1):
                    eng.wait_ge(rs0_ok, g + 1)
                    for b in range(GB):
                        eng.tensor_scalar(xn[:, b, :], xn[:, b, :], mv0[:, b, 0:1], rs0[:, b:b + 1],
                                          ALU.subtract, ALU.mult).then_inc(x1_ok, 1)
                elif u[0] == "D":
                    c = u[1]
                    eng.wait_ge(x1T_hi_ok, g * DC + c + 1)
                    eng.tensor_tensor(hT_lo[:, c, :], d_banks[c][:, :], hT_hi[:, c, :].bitcast(F32),
                                      ALU.subtract).then_inc(x1T_lo_ok, 1)
                elif u[0] == "N":
                    l, k = u[1], u[2]
                    m, side = divmod(k, 2)
                    eng.wait_ge(n_hi_ok, h * (2 * DC * L) + 2 * DC * l + k + 1)
                    eng.tensor_tensor(nT_lo[:, m % 2, side, :], nh_bank(l, k)[:, :],
                                      nT_hi[:, m % 2, side, :].bitcast(F32), ALU.subtract).then_inc(n_lo_ok, 1)
                elif u[0] == "H":
                    l, b = u[1], u[2]
                    eng.wait_ge(hl_mm, h * (GB * L) + GB * l + b + 1)
                    if some(n := h * (GB * L) + GB * (l - 1) + b + 1):
                        eng.wait_ge(c_mm, n)
                    eng.tensor_tensor(hl[:, b, 0:D], nh_bank(l, b)[:, 0:D], blin_b[:, l, :], ALU.add).then_inc(hl_sb, 1)
                elif u[0] == "M":
                    l, p = u[1], u[2]
                    eng.wait_ge(u_mm, h * (L * DC) + DC * (l + 1))
                    eng.wait_ge(tri_ok, (h + 1) * 2)
                    if some(n := h * (2 * L) + 2 * l + p):
                        eng.wait_ge(ut_ok, n)
                    eng.tensor_tensor(uw[:, :, :, :], u_banks[p][:, :].rearrange("p (b s n) -> p b s n", b=2, s=2),
                                      tri[:, 2 * p:2 * p + 2, :, :], ALU.mult).then_inc(u_sb, 1)
                    eng.wait_ge(u_sb, h * (2 * L) + 2 * l + p + 1)
                    if some(n := h * (GB * L) + GB * (l - 1) + 2 * p + 2):
                        eng.wait_ge(c_mm, n)
                    eng.tensor_tensor(uc[:, 2 * p:2 * p + 2, :], uw[:, :, 0, :], uw[:, :, 1, :],
                                      ALU.add).then_inc(ut_ok, 1)
                elif u[0] == "E":
                    l, p = u[1], u[2]
                    eng.wait_ge(ue_ok, h * (2 * L) + 2 * l + p + 1)
                    eng.tensor_tensor(uc[:, 2 * p:2 * p + 2, :], uc[:, 2 * p:2 * p + 2, :],
                                      adjT[:, 2 * p:2 * p + 2, :], ALU.mult).then_inc(e_ok, 1)
                elif u[0] == "C":
                    l, b = u[1], u[2]
                    eng.wait_ge(c_sb, h * (GB * L) + GB * l + b + 1)
                    eng.bn_stats(st1[:, b, :], cs[:, b, 0:D]).then_inc(st1_ok, 1)
                elif u == ("Y", 0):
                    context_stats(0, h)
                elif u == ("Y", 1):
                    context_scale(0, h)
                elif u[0] == "Y":
                    b = u[1] - 2
                    eng.wait_ge(sc_ok, h * (4 * L) + 4)
                    eng.tensor_scalar(cs[:, b, 0:D], cs[:, b, 0:D], mv1[:, b, 0:1], sc[:, 4, b:b + 1],
                                      ALU.subtract, ALU.mult).then_inc(y_ok, 1)
                elif u == ("F", 0):
                    context_stats(L - 1, h)
                elif u == ("F", 1):
                    context_scale(L - 1, h)
                elif u[0] == "F" and u[1] < 2 * GB + 2:
                    last_layer(h, *divmod(u[1] - 2, 2))
                elif u[0] == "F":
                    last_norm(h, u[1] - (2 * GB + 2))
                elif u[0] == "W":
                    c = u[1]
                    eng.wait_ge(h1_ok, h * DC + c + 1)
                    eng.wait_ge(hl_mm, h * (L * GB) + GB)
                    eng.wait_ge(u_mm, h * (L * DC) + DC)
                    eng.tensor_copy(hT_hi[:, c, :], x_pr[:, c, :]).then_inc(h1_hi_ok, 1)

            def stats0(g, b):
                eng.wait_ge(res0_ok, g * GB + b + 1)
                eng.bn_stats(st0[:, b, :], xn[:, b, :]).then_inc(st0_ok, 1)

            def context_stats(l, h):
                eng.wait_ge(st1_ok, h * (GB * L) + GB * l + GB)
                alone(eng)
                for b in range(GB):
                    last = eng.bn_aggr(mv1[:, b, :], st1[:, b, :])
                last.then_inc(mv1_ok, 1)
                eng.wait_ge(mv1_ok, h * L + l + 1)
                eng.tensor_scalar(sc[:, 0, :], mv1[:, :, 1], float(D) / (D - 1), None, ALU.mult).then_inc(sc_ok, 1)
                eng.tensor_scalar(sc[:, 2, :], cs[:, :, D], SUM_EPS, None, ALU.add).then_inc(sc_ok, 1)

            def context_scale(l, h):
                eng.wait_ge(sc_ok, h * (4 * L) + 4 * l + 2)
                eng.wait_ge(sd_ok, h * L + l + 1)
                eng.scalar_tensor_tensor(out=sc[:, 3, :], in0=sc[:, 2, :], scalar=L1_EPS, in1=sc[:, 1, :],
                                         op0=ALU.mult, op1=ALU.add).then_inc(sc_ok, 1)
                eng.wait_ge(sc_ok, h * (4 * L) + 4 * l + 3)
                eng.reciprocal(sc[:, 4, :], sc[:, 3, :]).then_inc(sc_ok, 1)

            def last_layer(h, b, step):
                if step == 0:
                    eng.wait_ge(sc_ok, (h + 1) * (4 * L))
                    eng.scalar_tensor_tensor(out=cs[:, b, 0:D], in0=cs[:, b, 0:D], scalar=mv1[:, b, 0:1],
                                             in1=lna_b[:, :], op0=ALU.subtract, op1=ALU.mult).then_inc(fa_ok, 1)
                    eng.wait_ge(fa_ok, h * GB + b + 1)
                    eng.scalar_tensor_tensor(out=cs[:, b, 0:D], in0=cs[:, b, 0:D], scalar=sc[:, 4, b:b + 1],
                                             in1=lnb_b[:, :], op0=ALU.mult, op1=ALU.add).then_inc(fb_ok, 1)
                else:
                    eng.wait_ge(fb_ok, h * GB + b + 1)
                    eng.wait_ge(ld_x1, (h + 1) * 16)
                    eng.scalar_tensor_tensor(out=cs[:, b, 0:D], in0=cs[:, b, 0:D], scalar=0.0,
                                             in1=x1[:, b, :], op0=ALU.max, op1=ALU.add).then_inc(res1_ok, 1)
                    eng.wait_ge(res1_ok, h * GB + b + 1)
                    eng.bn_stats(stf[:, b, :], cs[:, b, 0:D]).then_inc(stf_ok, 1)

            def last_norm(h, step):
                if step == 0:
                    eng.wait_ge(stf_ok, (h + 1) * GB)
                    alone(eng)
                    for b in range(GB):
                        last = eng.bn_aggr(mvf[:, b, :], stf[:, b, :])
                    last.then_inc(mvf_ok, 1)
                    eng.wait_ge(mvf_ok, h + 1)
                    eng.tensor_scalar(rsf[:, 0, :], mvf[:, :, 1], LN_EPS, None, ALU.add).then_inc(vef_ok, 1)
                else:
                    eng.wait_ge(rsf_ok, h + 1)
                    for b in range(GB):
                        eng.tensor_scalar(cs[:, b, 0:D], cs[:, b, 0:D], mvf[:, b, 0:1], rsf[:, 1, b:b + 1],
                                          ALU.subtract, ALU.mult).then_inc(out_ok, 1)

            eng.wait_ge(zeros, 1)
            for kz in (kz_hi, kz_lo):
                for slot in range(2):
                    eng.tensor_copy(kz[:, slot, :, :], bias[:, :, :]).then_inc(kz_zero, 1)
            for i in range(3):
                eng.wait_ge(ld_w0s[i], 16)
                eng.tensor_copy(w0_hi[:, i, :, :], w0_stage[i]).then_inc(w0_hi_done, 1)
                eng.wait_ge(w0_hi_done, i + 1)
                eng.tensor_tensor(w0_lo[:, i, :, :], w0_stage[i], w0_hi[:, i, :, :].bitcast(F32),
                                  ALU.subtract).then_inc(w0_lo_done, 1)
            eng.wait_ge(ld_w0, 4 * 16)
            eng.wait_ge(kz_zero, 4)
            over_turns(eng, unit)

        @block.tensor
        def _(eng):
            def split_product(out, w_hi, w_lo, x_hi, x_lo):
                for c in range(DC):
                    for n, (a, b) in enumerate(((w_hi, x_hi), (w_hi, x_lo), (w_lo, x_hi))):
                        last = eng.matmul(out, a(c), b(c), start=(c == 0 and n == 0), stop=(c == DC - 1 and n == 2))
                return last

            def unit(u, g):
                h = g
                if u[0] == "A":
                    i, m = divmod(u[1], DC)
                    if isinstance(g, int) and g == 0:
                        eng.wait_ge(w0_lo_done, i + 1)
                    if u[1] == 0:
                        eng.wait_ge(xT_lo_ok, (g + 1) * DC)
                        if some(n := g * GB):
                            eng.wait_ge(v_sb, n)
                        if some(n := g * NQ):
                            eng.wait_ge(s_sb, n)
                    elif u[1] - 2 >= DC:
                        eng.wait_ge(qk_sb, g * (2 * DC) + u[1] - 1)
                    elif u[1] > 1:
                        eng.wait_ge(q_lo_ok, g * DC + u[1] - 1)
                    cols = slice(m * P, (m + 1) * P)
                    split_product(proj_banks[u[1] % 2][:, :],
                                  lambda c: w0_hi[:, i, c, cols], lambda c: w0_lo[:, i, c, cols],
                                  lambda c: xT_hi[:, c, :], lambda c: xT_lo[:, c, :]).then_inc(qk_mm, 1)
                elif u[0] == "B":
                    b = u[1]
                    if b < 2:
                        eng.wait_ge(qk_sb, (g + 1) * (2 * DC) - 1 + b)
                    else:
                        eng.wait_ge(v_sb, g * GB + b - 1)
                    if isinstance(g, int) and g == 0:
                        eng.wait_ge(w0_lo_done, 3)
                    rows = slice(b * N, (b + 1) * N)
                    split_product(proj_banks[b % 2][:, 0:D],
                                  lambda c: xT_hi[:, c, rows], lambda c: xT_lo[:, c, rows],
                                  lambda c: w0_hi[:, 2, c, :], lambda c: w0_lo[:, 2, c, :]).then_inc(v_mm, 1)
                elif u[0] == "S":
                    q = u[1]
                    b, c = divmod(q, DC)
                    eng.wait_ge(kz_lo_ok, g * (NQ * HPC) + HPC * (q + 1))
                    if some(n := g * NQ + q - 1):
                        eng.wait_ge(s_sb, n)
                    if q == 0:
                        eng.wait_ge(q_lo_ok, (g + 1) * DC)
                        if some(n := g * DC):
                            eng.wait_ge(x1T_lo_ok, n)
                    elif q == 1:
                        eng.wait_ge(v_sb, (g + 1) * GB - 1)
                    elif q == 2:
                        eng.wait_ge(v_sb, (g + 1) * GB)
                    rows = slice(b * N, (b + 1) * N)
                    eng.matmul(bank_s[q % 2][:, :], qT_hi[:, c, rows], kz_hi[:, q % 2, :, :], start=True, stop=False)
                    eng.matmul(bank_s[q % 2][:, :], qT_lo[:, c, rows], kz_hi[:, q % 2, :, :], start=False, stop=False)
                    eng.matmul(bank_s[q % 2][:, :], qT_hi[:, c, rows], kz_lo[:, q % 2, :, :],
                               start=False, stop=True).then_inc(s_mm, 1)
                elif u[0] == "T":
                    q = u[1]
                    eng.wait_ge(exp_ok, g * NQ + q + 1)
                    if some(n := g * NQ + q):
                        eng.wait_ge(pt_sb, n)
                    for c in range(HPC):
                        last = eng.transpose(bank_t[:, c * N:(c + 1) * N], pr[:, q % 3, c, :], ident[:, :])
                    last.then_inc(pt_mm, 1)
                elif u[0] == "V":
                    q = u[1]
                    b, c = divmod(q, DC)
                    eng.wait_ge(pt_sb, g * NQ + q + 1)
                    eng.wait_ge(v_sb, g * GB + b + 1)
                    if c == 0:
                        if some(n := g * GB + b):
                            eng.wait_ge(att_ok, n)
                    for j in range(HPC):
                        hh = c * HPC + j
                        last = eng.matmul(bank_o[:, hh * VW:(hh + 1) * VW], prT[:, q % 2, j, :], v[:, b, hh, :],
                                          start=True, stop=True)
                    last.then_inc(o_mm, 1)
                elif u[0] == "D":
                    c = u[1]
                    if c == 0:
                        eng.wait_ge(pt_sb, (g + 1) * NQ)
                    elif c == 1:
                        eng.wait_ge(att_ok, (g + 1) * GB)
                    else:
                        eng.wait_ge(s_sb, (g + 1) * NQ)
                    for b in range(GB):
                        eng.wait_ge(x1_ok, g * GB + b + 1)
                        last = eng.transpose(d_banks[c][:, b * N:(b + 1) * N], xn[:, b, c * P:(c + 1) * P], ident[:, :])
                    last.then_inc(x1T_mm, 1)
                elif u[0] == "N":
                    l, k = u[1], u[2]
                    m, side = divmod(k, 2)
                    if l == 0:
                        if k == 0:
                            eng.wait_ge(x1T_lo_ok, (h + 1) * DC)
                            if some(n := h * (GB * L)):
                                eng.wait_ge(c_sb, n)
                    elif k == 0:
                        eng.wait_ge(h1_lo_ok, (h + 1) * DC)
                    if k >= 2:
                        eng.wait_ge(n_lo_ok, h * (2 * DC * L) + 2 * DC * l + k - 1)
                    if isinstance(h, int) and h == 0:
                        eng.wait_ge(w1_lo_done, 3 * L)
                    cols = slice(m * P, (m + 1) * P)
                    split_product(nh_bank(l, k)[:, :],
                                  lambda c: w1_hi[:, l, side, c, cols], lambda c: w1_lo[:, l, side, c, cols],
                                  lambda c: hT_hi[:, c, :], lambda c: hT_lo[:, c, :]).then_inc(n_mm, 1)
                elif u[0] == "H":
                    l, b = u[1], u[2]
                    if b < 2:
                        eng.wait_ge(n_lo_ok, h * (2 * DC * L) + 2 * DC * (l + 1) - 1 + b)
                    else:
                        eng.wait_ge(hl_sb, h * (GB * L) + GB * l + b - 1)
                    rows = slice(b * N, (b + 1) * N)
                    split_product(nh_bank(l, b)[:, 0:D],
                                  lambda c: hT_hi[:, c, rows], lambda c: hT_lo[:, c, rows],
                                  lambda c: w1_hi[:, l, 2, c, :], lambda c: w1_lo[:, l, 2, c, :]).then_inc(hl_mm, 1)
                elif u[0] == "U":
                    l, m = u[1], u[2]
                    eng.wait_ge(n_lo_ok, h * (2 * DC * L) + 2 * DC * l + 2 * (m + 1))
                    if m == 0:
                        if l == 0:
                            if some(n := h * (2 * L)):
                                eng.wait_ge(u_sb, n)
                        else:
                            eng.wait_ge(h1_ok, (h + 1) * DC)
                    for b in range(GB):
                        rows = slice(b * N, (b + 1) * N)
                        for n, (x, y) in enumerate(((hT_hi, nT_hi), (hT_lo, nT_hi), (hT_hi, nT_lo))):
                            last = eng.matmul(u_banks[b // 2][:, (b % 2) * 2 * N:(b % 2 + 1) * 2 * N],
                                              x[:, m, rows], y[:, m % 2, :, rows],
                                              start=(m == 0 and n == 0 and b % 2 == 0),
                                              stop=(m == DC - 1 and n == 2 and b % 2 == 1))
                    last.then_inc(u_mm, 1)
                elif u[0] == "C":
                    l, b = u[1], u[2]
                    eng.wait_ge(e_ok, h * (2 * L) + 2 * l + b // 2 + 1)
                    eng.wait_ge(hl_sb, h * (GB * L) + GB * (l + 1))
                    if b >= 2:
                        eng.wait_ge(c_sb, h * (GB * L) + GB * l + b - 1)
                    eng.matmul(c_banks[b % 2][:, 0:D + 1], uc[:, b, :], hl[:, b, :], start=True, stop=True).then_inc(c_mm, 1)
                elif u[0] == "W":
                    c = u[1]
                    if c == 0:
                        eng.wait_ge(u_sb, h * (2 * L) + 2)
                    elif c == 1:
                        eng.wait_ge(c_sb, h * (GB * L) + GB)
                    for b in range(GB):
                        eng.wait_ge(y_ok, h * GB + b + 1)
                        last = eng.transpose(w_banks[c][:, b * N:(b + 1) * N], cs[:, b, c * P:(c + 1) * P], ident[:, :])
                    last.then_inc(yT_mm, 1)

            eng.wait_ge(const_done, 5)
            over_turns(eng, unit)


_OUT = ("out_dram", (G, P, GB, D))


def kernel(**inputs):
    import concourse.bacc as _bacc
    from concourse import mybir as _mybir
    from concourse.bass_utils import run_bass_kernel_spmd as _run

    a = {k: np.ascontiguousarray(x) for k, x in inputs.items()}
    x, adj = a["x"], a["adj"]
    grouped = x.reshape(G, GB, N, D)
    pairs = adj.reshape(G, GB, N, N)

    def columns(b):
        return b.reshape(DC, P).T

    arrays = {
        "xT_in": grouped.reshape(G, T, DC, P).transpose(0, 3, 2, 1),
        "xn_in": grouped.transpose(0, 2, 1, 3),
        "adj_in": pairs.transpose(0, 2, 1, 3),
        "adjT_in": pairs.transpose(0, 3, 1, 2),
        "wq_in": a["L0_gnn_Wq"], "wk_in": a["L0_gnn_Wk"], "wv_in": a["L0_gnn_Wv"],
        "bq_in": columns(a["L0_gnn_bq"]), "bk_in": columns(a["L0_gnn_bk"]), "bv_in": a["L0_gnn_bv"],
        "beta_in": a["L0_gnn_beta"].reshape(1),
        "wl_in": a["L1_gnn_W_left"], "wr_in": a["L1_gnn_W_right"],
        "wlin_in": a["L1_gnn_W_lin"].transpose(0, 2, 1),
        "blin_in": a["L1_gnn_b_lin"],
        "lna_col_in": columns(a["L1_gnn_ln_a"][0]), "lnb_col_in": columns(a["L1_gnn_ln_b"][0]),
        "lna_in": a["L1_gnn_ln_a"][1], "lnb_in": a["L1_gnn_ln_b"][1],
    }
    arrays = {k: np.ascontiguousarray(w) for k, w in arrays.items()}
    nc = _bacc.Bacc("TRN2", target_bir_lowering=False, num_devices=1)
    args = [nc.dram_tensor(k, w.shape, _mybir.dt.from_np(w.dtype), kind="ExternalInput").ap() for k, w in arrays.items()]
    args.append(nc.dram_tensor(_OUT[0], _OUT[1], F32, kind="ExternalOutput").ap())
    graph_blocks(nc, *args)
    r = _run(nc, [arrays], core_ids=[0])
    got = r.results[0][_OUT[0]]
    return np.ascontiguousarray(got.transpose(0, 2, 1, 3)).reshape(NB, N, D)
```
